# Optimizing a Trainium2 kernel written in Bass

```python
import numpy as np
import jax
import jax.numpy as jnp

def _softmax(x, axis=-1):
    return jax.nn.softmax(x, axis=axis)

def _gelu(x):
    return jax.nn.gelu(x, approximate=True)

def _silu(x):
    return jax.nn.silu(x)

def _sigmoid(x):
    return jax.nn.sigmoid(x)

def _layernorm(x, axis=-1, eps=1e-05):
    m = jnp.mean(x, axis=axis, keepdims=True)
    v = jnp.var(x, axis=axis, keepdims=True)
    return (x - m) / jnp.sqrt(v + eps)

def _scatter_add(tgt, idx, src, axis=0):
    return tgt.at[idx].add(src)

def _segment_sum(src, seg, n):
    return jax.ops.segment_sum(src, seg, n)
kernel_name = 'mk_seq_postln_d2_jaxref_r4_8d3733'

def setup_inputs(seed: int=0):
    np.random.seed(seed)
    _w = jnp.asarray

    def _L0_attn_setup():
        import math
        import jax, jax.numpy as jnp
        import numpy as np
        D_MODEL = 256
        N_HEADS = 16
        D_K = D_MODEL // N_HEADS
        THETA = 10000.0

        def _rope(t, cos, sin):
            B, H, S, d = t.shape
            tp = t.reshape(B, H, S, d // 2, 2)
            even, odd = (tp[..., 0], tp[..., 1])
            r_even = even * cos - odd * sin
            r_odd = even * sin + odd * cos
            return jnp.stack([r_even, r_odd], axis=-1).reshape(B, H, S, d)
        key = jax.random.key(seed)
        k1, k2, k3 = jax.random.split(key, 3)
        B, S = (2, 512)
        x = jax.random.normal(k1, (B, S, D_MODEL), dtype=jnp.float32)
        std_qkv = math.sqrt(2.0 / (D_MODEL + 3 * D_MODEL))
        std_out = math.sqrt(2.0 / (D_MODEL + D_MODEL))
        w_qkv = jnp.clip(jax.random.normal(k2, (3 * D_MODEL, D_MODEL), dtype=jnp.float32) * std_qkv, -3 * std_qkv, 3 * std_qkv)
        b_qkv = jnp.zeros((3 * D_MODEL,), dtype=jnp.float32)
        w_out = jnp.clip(jax.random.normal(k3, (D_MODEL, D_MODEL), dtype=jnp.float32) * std_out, -3 * std_out, 3 * std_out)
        b_out = jnp.zeros((D_MODEL,), dtype=jnp.float32)
        return {'x': x, 'w_qkv': w_qkv, 'b_qkv': b_qkv, 'w_out': w_out, 'b_out': b_out}
    _L0_attn_in = _L0_attn_setup()

    def _L0_ffn_setup():
        import jax, jax.numpy as jnp
        import numpy as np
        TOP_K = 4
        key = jax.random.key(seed)
        ks = jax.random.split(key, 6)
        B, S, H, I, E = (2, 256, 256, 256, 16)
        SD = I * 1
        s = 0.02
        return {'hidden_states': jax.random.normal(ks[0], (B, S, H), jnp.float32), 'gate_w': jax.random.normal(ks[1], (E, H), jnp.float32) * s, 'w1': jax.random.normal(ks[2], (E, I, H), jnp.float32) * s, 'w2': jax.random.normal(ks[3], (E, H, I), jnp.float32) * s, 'shared_gu': jax.random.normal(ks[4], (2 * SD, H), jnp.float32) * s, 'shared_down': jax.random.normal(ks[5], (H, SD), jnp.float32) * s}
    _L0_ffn_in = _L0_ffn_setup()

    def _L1_attn_setup():
        import jax, jax.numpy as jnp
        import numpy as np
        B, S, H, NH = (4, 512, 256, 16)
        HD = H // NH
        key = jax.random.key(seed)
        ks = jax.random.split(key, 9)
        s = 1.0 / np.sqrt(H)
        return {'hidden_state': jax.random.normal(ks[0], (B, S, H), dtype=jnp.float32), 'Wq': jax.random.normal(ks[1], (H, H), dtype=jnp.float32) * s, 'bq': jnp.zeros((H,), dtype=jnp.float32), 'Wk': jax.random.normal(ks[2], (H, HD), dtype=jnp.float32) * s, 'bk': jnp.zeros((HD,), dtype=jnp.float32), 'Wv': jax.random.normal(ks[3], (H, HD), dtype=jnp.float32) * s, 'bv': jnp.zeros((HD,), dtype=jnp.float32), 'Wo': jax.random.normal(ks[4], (H, H), dtype=jnp.float32) * s, 'bo': jnp.zeros((H,), dtype=jnp.float32)}
    _L1_attn_in = _L1_attn_setup()

    def _L1_ffn_setup():
        import jax, jax.numpy as jnp
        import numpy as np
        B, S, H, I, E = (2, 1024, 256, 128, 8)
        key = jax.random.key(seed)
        ks = jax.random.split(key, 5)
        scale_h = 1.0 / np.sqrt(H)
        scale_i = 1.0 / np.sqrt(I)
        return {'hidden_states': jax.random.normal(ks[0], (B, S, H), dtype=jnp.float32), 'gate_w': jax.random.normal(ks[1], (E, H), dtype=jnp.float32) * scale_h, 'w_gate': jax.random.normal(ks[2], (E, I, H), dtype=jnp.float32) * scale_h, 'w_up': jax.random.normal(ks[3], (E, I, H), dtype=jnp.float32) * scale_h, 'w_down': jax.random.normal(ks[4], (E, H, I), dtype=jnp.float32) * scale_i}
    _L1_ffn_in = _L1_ffn_setup()
    _d = {'L0_attn_x': _L0_attn_in['x'], 'L0_attn_w_qkv': _L0_attn_in['w_qkv'], 'L0_attn_b_qkv': _L0_attn_in['b_qkv'], 'L0_attn_w_out': _L0_attn_in['w_out'], 'L0_attn_b_out': _L0_attn_in['b_out'], 'L0_ffn_gate_w': _L0_ffn_in['gate_w'], 'L0_ffn_w1': _L0_ffn_in['w1'], 'L0_ffn_w2': _L0_ffn_in['w2'], 'L0_ffn_shared_gu': _L0_ffn_in['shared_gu'], 'L0_ffn_shared_down': _L0_ffn_in['shared_down'], 'L1_attn_Wq': _L1_attn_in['Wq'], 'L1_attn_bq': _L1_attn_in['bq'], 'L1_attn_Wk': _L1_attn_in['Wk'], 'L1_attn_bk': _L1_attn_in['bk'], 'L1_attn_Wv': _L1_attn_in['Wv'], 'L1_attn_bv': _L1_attn_in['bv'], 'L1_attn_Wo': _L1_attn_in['Wo'], 'L1_attn_bo': _L1_attn_in['bo'], 'L1_ffn_gate_w': _L1_ffn_in['gate_w'], 'L1_ffn_w_gate': _L1_ffn_in['w_gate'], 'L1_ffn_w_up': _L1_ffn_in['w_up'], 'L1_ffn_w_down': _L1_ffn_in['w_down']}
    _x0 = _d['L0_attn_x']
    _d['L0_attn_x'] = jax.random.normal(jax.random.fold_in(jax.random.key(seed), 1), (16, 512, 256), dtype=_x0.dtype)
    del _x0
    return _d

def reference(L0_attn_x, L0_attn_w_qkv, L0_attn_b_qkv, L0_attn_w_out, L0_attn_b_out, L0_ffn_gate_w, L0_ffn_w1, L0_ffn_w2, L0_ffn_shared_gu, L0_ffn_shared_down, L1_attn_Wq, L1_attn_bq, L1_attn_Wk, L1_attn_bk, L1_attn_Wv, L1_attn_bv, L1_attn_Wo, L1_attn_bo, L1_ffn_gate_w, L1_ffn_w_gate, L1_ffn_w_up, L1_ffn_w_down):

    def _L0_attn_ref(x, w_qkv, b_qkv, w_out, b_out):
        import math
        import jax, jax.numpy as jnp
        import numpy as np
        D_MODEL = 256
        N_HEADS = 16
        D_K = D_MODEL // N_HEADS
        THETA = 10000.0

        def _rope(t, cos, sin):
            B, H, S, d = t.shape
            tp = t.reshape(B, H, S, d // 2, 2)
            even, odd = (tp[..., 0], tp[..., 1])
            r_even = even * cos - odd * sin
            r_odd = even * sin + odd * cos
            return jnp.stack([r_even, r_odd], axis=-1).reshape(B, H, S, d)
        B, S, _ = x.shape
        qkv = jnp.einsum('bsi,oi->bso', x, w_qkv) + b_qkv
        qkv = qkv.reshape(B, S, 3, N_HEADS, D_K).transpose(2, 0, 3, 1, 4)
        q, k, v = (qkv[0], qkv[1], qkv[2])
        inv_freq = THETA ** (-jnp.arange(0, D_K, 2, dtype=jnp.float32) / D_K)
        ang = jnp.arange(S, dtype=jnp.float32)[:, None] * inv_freq[None, :]
        cos, sin = (jnp.cos(ang), jnp.sin(ang))
        q = _rope(q, cos, sin)
        k = _rope(k, cos, sin)
        scale = 1.0 / math.sqrt(D_K)
        scores = jnp.einsum('bhqd,bhkd->bhqk', q.astype(jnp.float32), k.astype(jnp.float32)) * scale
        causal = jnp.tril(jnp.ones((S, S), dtype=bool))
        scores = jnp.where(causal, scores, jnp.finfo(jnp.float32).min)
        ex = jnp.exp(scores - jnp.max(scores, axis=-1, keepdims=True))
        attn = ex / (jnp.sum(ex, axis=-1, keepdims=True) + 1e-08)
        attn = attn.astype(v.dtype)
        o = jnp.einsum('bhqk,bhkd->bhqd', attn, v)
        o = o.transpose(0, 2, 1, 3).reshape(B, S, D_MODEL)
        out = jnp.einsum('bsi,oi->bso', o, w_out) + b_out
        return out

    def _L0_ffn_ref(hidden_states, gate_w, w1, w2, shared_gu, shared_down):
        import jax, jax.numpy as jnp
        import numpy as np
        TOP_K = 4
        orig_shape = hidden_states.shape
        H = orig_shape[-1]
        x = hidden_states.reshape(-1, H)
        T = x.shape[0]
        E = gate_w.shape[0]
        logits = x @ gate_w.T
        probs = jax.nn.softmax(logits, axis=-1)
        topv, topi = jax.lax.top_k(probs, TOP_K)
        topv = topv / jnp.sum(topv, axis=-1, keepdims=True)
        W = jnp.zeros((T, E), x.dtype).at[jnp.arange(T)[:, None], topi].set(topv)
        h = jax.nn.silu(jnp.einsum('th,eih->tei', x, w1))
        routed = jnp.einsum('tei,ehi,te->th', h, w2, W)
        gu = x @ shared_gu.T
        gate, up = jnp.split(gu, 2, axis=-1)
        shared = jax.nn.silu(gate) * up @ shared_down.T
        return (routed + shared).reshape(orig_shape)

    def _L1_attn_ref(hidden_state, Wq, bq, Wk, bk, Wv, bv, Wo, bo):
        import jax, jax.numpy as jnp
        import numpy as np
        B, S, H, NH = (4, 512, 256, 16)
        HD = H // NH
        b, s = (hidden_state.shape[0], hidden_state.shape[1])
        q = hidden_state @ Wq + bq
        k = hidden_state @ Wk + bk
        v = hidden_state @ Wv + bv
        q = q.reshape(b, s, NH, HD).transpose(0, 2, 1, 3)
        scale = 1.0 / jnp.sqrt(jnp.float32(HD))
        scores = jnp.einsum('bhqd,bkd->bhqk', q, k) * scale
        probs = jax.nn.softmax(scores, axis=-1)
        out = jnp.einsum('bhqk,bkd->bhqd', probs, v)
        out = out.transpose(0, 2, 1, 3).reshape(b, s, NH * HD)
        return out @ Wo + bo

    def _L1_ffn_ref(hidden_states, gate_w, w_gate, w_up, w_down):
        import jax, jax.numpy as jnp
        import numpy as np
        B, S, H, I, E = (2, 1024, 256, 128, 8)
        b, s, h = hidden_states.shape
        x = hidden_states.reshape(-1, h)
        logits = x @ gate_w.T
        top_v = jnp.max(logits, axis=-1)
        sel = jnp.argmax(logits, axis=-1)
        rw = jax.nn.sigmoid(top_v)
        out = jnp.zeros_like(x)
        n_exp = gate_w.shape[0]
        for e in range(n_exp):
            mask = (sel == e).astype(x.dtype)
            xs = x * (rw * mask)[:, None]
            g = xs @ w_gate[e].T
            u = xs @ w_up[e].T
            out = out + u * jax.nn.silu(g) @ w_down[e].T
        return out.reshape(b, s, h)
    x = L0_attn_x
    x = _layernorm(x + _L0_attn_ref(x, L0_attn_w_qkv, L0_attn_b_qkv, L0_attn_w_out, L0_attn_b_out), axis=-1)
    x = _layernorm(x + _L0_ffn_ref(x, L0_ffn_gate_w, L0_ffn_w1, L0_ffn_w2, L0_ffn_shared_gu, L0_ffn_shared_down), axis=-1)
    x = _layernorm(x + _L1_attn_ref(x, L1_attn_Wq, L1_attn_bq, L1_attn_Wk, L1_attn_bk, L1_attn_Wv, L1_attn_bv, L1_attn_Wo, L1_attn_bo), axis=-1)
    x = _layernorm(x + _L1_ffn_ref(x, L1_ffn_gate_w, L1_ffn_w_gate, L1_ffn_w_up, L1_ffn_w_down), axis=-1)
    return x

_drawn_inputs = setup_inputs


def setup_inputs(seed=0):
    import zlib

    import numpy as np

    out = dict(_drawn_inputs(seed))
    spreads = {'L0_attn_b_qkv': (0.0, 0.1),
     'L0_attn_b_out': (0.0, 0.1),
     'L1_attn_bq': (0.0, 0.1),
     'L1_attn_bk': (0.0, 0.1),
     'L1_attn_bv': (0.0, 0.1),
     'L1_attn_bo': (0.0, 0.1)}
    factors = {}
    for name, (base, spread) in spreads.items():
        noise = np.random.default_rng([zlib.crc32(name.encode()), seed]).standard_normal(out[name].shape)
        drawn = base * np.exp(spread * noise) if base else spread * noise
        out[name] = jnp.asarray(drawn.astype(out[name].dtype))
    for name, factor in factors.items():
        out[name] = (out[name] * factor).astype(out[name].dtype)
    return out
```

```python
from contextlib import ExitStack

import numpy as np

import concourse.bass as bass
from concourse import mybir

F32, F32R, BF16 = mybir.dt.float32, mybir.dt.float32r, mybir.dt.bfloat16
ALU, ACT, AX = mybir.AluOpType, mybir.ActivationFunctionType, mybir.AxisListType

P = 128
NB, S, D = 16, 512, 256
H, HD = 16, 16
TB = S // P
KC = D // P
HALF = HD // 2
GROUPS, GH = 4, 4
SPLITS = 3
STACK = SPLITS * HD
ROWS = STACK + 2
LEAD = 7
SCALE = 1.0 / float(np.sqrt(HD))
LN_EPS, SUM_EPS = 1e-5, 1e-8
MASKED = -3.0e38
DMA = 16


def at(eng, sem, value):
    if not isinstance(value, int) or value > 0:
        eng.wait_ge(sem, value)


def at_most(value, most):
    return min(value, most) if isinstance(value, int) else value


def at_alone(eng, sem, value, passed):
    at(eng, sem, value)
    if not isinstance(value, int):
        eng.sem_inc(passed, 1)


class Chain:

    def __init__(self, eng, sem, per_two):
        self.eng, self.sem, self.n, self.per_two = eng, sem, 0, per_two

    def then(self, instruction, alone=None):
        self.n = self.n + 1
        instruction.then_inc(self.sem, 1)
        if alone:
            at_alone(self.eng, self.sem, self.n, alone)
        else:
            self.eng.wait_ge(self.sem, self.n)


def over_batches(eng, body, first, looped, last, chain=None):
    lo, hi = looped
    for b in range(first, lo):
        body(b)
    before = chain.n if chain else 0
    with eng.Fori(0, (hi - lo) // 2) as i:
        if chain:
            chain.n = i * chain.per_two + before
        body(i * 2 + lo, 0)
        body(i * 2 + (lo + 1), 1)
    if chain:
        chain.n = before + (hi - lo) // 2 * chain.per_two
    for b in range(hi, last + 1):
        body(b)


def exists(b):
    return not isinstance(b, int) or 0 <= b < NB


def spread(ap, dims):
    return bass.AP(ap.tensor, ap.offset, [list(ap.ap[0])] + dims)


def product(pe, out, a, b, start=True, stop=True):
    pe.matmul(out, a[0], b[0], start=start, stop=False)
    pe.matmul(out, a[1], b[0], start=False, stop=False)
    return pe.matmul(out, a[0], b[1], start=False, stop=stop)


def load_split_weights(nc, sems, specs, stage, name):
    landed = sems.enter_context(nc.semaphore(f"{name}_weights_landed"))
    hi_done = sems.enter_context(nc.semaphore(f"{name}_weights_hi"))
    lo_done = sems.enter_context(nc.semaphore(f"{name}_weights_lo"))
    half = stage.shape[1] // 2

    def staged(n, w):
        return stage[: w, (n % 2) * half:(n % 2) * half + size(n)]

    def size(n):
        return int(np.prod(specs[n][0].shape[1:]))

    with nc.Block() as block:
        @block.sync
        def _(sp):
            for n, (src, hi, lo) in enumerate(specs):
                at(sp, lo_done, n - 1)
                sp.dma_start(staged(n, src.shape[0]), src).then_inc(landed, DMA)
                sp.wait_ge(landed, DMA * (n + 1))

        @block.scalar
        def _(act):
            for n, (src, hi, lo) in enumerate(specs):
                act.wait_ge(landed, DMA * (n + 1))
                act.activation(hi, staged(n, src.shape[0]), ACT.Copy).then_inc(hi_done, 1)

        @block.vector
        def _(dve):
            for n, (src, hi, lo) in enumerate(specs):
                dve.wait_ge(hi_done, n + 1)
                dve.tensor_tensor(lo, staged(n, src.shape[0]), hi, ALU.subtract).then_inc(lo_done, 1)


def attention_layer(nc, sems, passed, name, causal, x_in, x_out, w_qkv, b_qkv, w_out, b_out, tables, ident_in):
    NQ = 4 if causal else 3
    NV = 2 if causal else 1
    NE = 3 if causal else 4
    PW = 1280 if causal else TB * S
    KVH = H if causal else 1
    parts = [(0, 0, 0, 0), (1, 0, 128, 1), (1, 384, 384, 3), (2, 0, 256, 2)] if causal else [
        (kb, 0, 0, kb) for kb in range(TB)]
    start_of = {kb: bank * S + col for bank, col, q0, kb in parts}
    width = {0: S, 1: S, 2: 256} if causal else {kb: S for kb in range(TB)}
    VC = D if causal else HD
    with ExitStack() as ctx:
        def sb(n, shape, dt=F32):
            return ctx.enter_context(nc.sbuf_tensor(f"{name}_{n}", shape, dt))

        def sem(n):
            return sems.enter_context(nc.semaphore(f"{name}_{n}"))

        q_dram = nc.dram_tensor(f"{name}_q_stacked", [NB, 2, HD, H, S], F32, kind="Internal").ap()
        k_dram = nc.dram_tensor(f"{name}_k_stacked", [NB, 2, HD, H, S], F32, kind="Internal").ap() if causal else None

        qs = sb("q_stack", [ROWS, H, S], F32R)
        ks = sb("k_stack", [ROWS, H if causal else 2, S], F32R)
        probs = sb("probs", [P, 2, GH, PW])
        vo = sb("v_ones", [P, 2, TB, KVH, 32])
        xn = sb("x_to_turn", [P, TB, D])
        xr = sb("x_residual", [P, TB, D])
        xt = [sb(f"xT_{p}", [P, KC, S], F32R) for p in ("hi", "lo")]
        qf = sb("q_projected", [P, 2, S])
        kf = sb("k_projected", [P, 2, S]) if causal else sb("k_projected", [HD, S])
        q_parts = sb("q_parts", [P, 2, 2, S], F32R)
        k_parts = sb("k_parts", [P, 2, 2, S], F32R) if causal else sb("k_parts", [HD, 2, S], F32R)
        mx = sb("row_max", [P, H * TB])
        mh = sb("max_parts", [GH * TB, 2, P], F32R)
        osb = sb("o_raw", [P, S])
        on = sb("o_normed", [P, TB, D])
        ot = [sb(f"oT_{p}", [P, KC, S], F32R) for p in ("hi", "lo")]
        den = sb("denominators", [P, 2, GH * TB])
        hb = sb("h", [P, 2, 2, D])
        stats = sb("stats", [P, 4, 6])
        mv = sb("mean_var", [P, 4, 2])
        veps = sb("var_eps", [P, 4])
        rstd = sb("rstd", [P, 4])
        mhalf = sb("minus_half", [P, 2])
        yo = sb("y_out", [P, TB, D])
        bo = sb("b_out", [P, D])
        ident = sb("identity", [P, P])
        QKC = 2 * D if causal else D + HD
        wqk = [sb(f"w_qk_{p}", [P, KC, QKC], F32R) for p in ("hi", "lo")]
        wv = [sb(f"w_v_{p}", [P, KC, VC], F32R) for p in ("hi", "lo")]
        wo = [sb(f"w_o_{p}", [P, KC, D], F32R) for p in ("hi", "lo")]
        bqk = sb("b_qk", [P, NQ])
        bv = sb("b_v", [P, VC])
        if causal:
            prods = sb("rope_products", [P, 4, S])
            rot = sb("rope_sums", [P, 2, S])
            cs = sb("cos_sin", [P, 2, S])
            mask = sb("causal_mask", [P, S], BF16)
            junk = sb("junk", [P, 2, S], BF16)

        def psum(n, banks):
            return ctx.enter_context(nc.psum_tensor(f"{name}_{n}", [P, banks, S], F32))

        m_ps = psum("ps_max", 2)
        e_ps = psum("ps_exp", NE)
        o_ps = psum("ps_o", 1)
        x0_ps = psum("ps_x0", 1)
        x1_ps = psum("ps_x1", 1) if causal else x0_ps

        const_landed, const_made = sem("const_landed"), sem("const_made")
        xn_landed, xr_landed, xr_biased = sem("xn_landed"), sem("xr_landed"), sem("xr_biased")
        q_written, k_written, max_landed = sem("q_written"), sem("k_written"), sem("max_landed")
        stack_landed = [sem(f"stack_landed_{g}") for g in range(GROUPS)]
        ks_landed, stored = sem("ks_landed"), sem("stored")
        m_scored, m_reduced, e_scored, e_exped, masked = (
            sem("m_scored"), sem("m_reduced"), sem("e_scored"), sem("e_exped"), sem("masked"))
        pv_done, o_evac, o_turned, o_normed = sem("pv_done"), sem("o_evac"), sem("o_turned"), sem("o_normed")
        mx_turned, mx_split = sem("mx_turned"), sem("mx_split")
        xt_turned, xt_hi, xt_split = sem("xt_turned"), sem("xt_hi"), sem("xt_split")
        qk_made, qk_evac, v_made, v_evac = sem("qk_made"), sem("qk_evac"), sem("v_made"), sem("v_evac")
        roped, summed = sem("roped"), sem("summed")
        q_hi, q_split, k_hi, k_split = sem("q_hi"), sem("q_split"), sem("k_hi"), sem("k_split")
        on_turned, on_hi, on_split = sem("on_turned"), sem("on_hi"), sem("on_split")
        y_made, y_evac, var_made, rstd_made, y_normed = (
            sem("y_made"), sem("y_evac"), sem("var_made"), sem("rstd_made"), sem("y_normed"))
        dve_order = sem("dve_order")
        dve_passed, pool_passed = passed

        stage = probs.rearrange("p a b c -> p (a b c)")[:, 0:4096]
        load_split_weights(nc, sems, [
            (w_qkv[0], *[w.rearrange("p c n -> p (c n)") for w in wqk]),
            (w_qkv[1], *[w.rearrange("p c n -> p (c n)") for w in wv]),
            (w_out, *[w.rearrange("p c n -> p (c n)") for w in wo]),
        ], stage, name)

        with nc.Block() as block:
            @block.sync
            def _(sp):
                loads = [(ident[:], ident_in), (bqk[:], b_qkv[0]), (bv[:], b_qkv[1]), (bo[:], b_out)]
                if causal:
                    loads += [(cs[:], tables[0])]
                for dst, src in loads:
                    sp.dma_start(dst, src).then_inc(const_landed, DMA)
                sp.wait_ge(const_landed, DMA * len(loads))

            @block.gpsimd
            def _(pool):
                pool.memset(mhalf[:], -0.5)
                pool.memset(vo[:], 0.0).then_inc(const_made, 1)
                pool.wait_ge(const_made, 1)
                pool.memset(vo[:, :, :, :, HD:HD + 1], 1.0)
                if causal:
                    pool.memset(mask[:], 0.0).then_inc(const_made, 1)
                    pool.wait_ge(const_made, 2)
                    pool.affine_select(out=mask[:], in_=mask[:], pattern=[[-1, S]], compare_op=ALU.is_ge,
                                       fill=MASKED, base=384, channel_multiplier=1)

            @block.vector
            def _(dve):
                dve.memset(ks[:].bitcast(F32), -1.0)

        def x_start(b, shared_bank):
            q = (qk_evac, at_most((b + 2) * NQ, NB * NQ))
            if isinstance(b, int) and b < 0:
                return q, q if shared_bank else (mx_split, 0)
            m = (mx_split, 1) if isinstance(b, int) and b == 0 else (o_normed, (b - 1) * GROUPS + 2)
            return (m, m) if shared_bank else (q, m)

        with nc.Block() as block:
            @block.tensor
            def _(pe):
                def body(b, par=None):
                    par = b % 2 if isinstance(b, int) else par
                    x0, x1 = x_start(b, not causal)
                    free = {"x0": x0, "x1": x1}

                    def bank(which, emptied):
                        k = which if causal else "x0"
                        at(pe, *free[k])
                        free[k] = emptied
                        return (x1_ps if which == "x1" else x0_ps)[:, 0, :]

                    for s in range(H):
                        g, j = divmod(s, GH)
                        bm, hm = (b, s + LEAD) if s + LEAD < H else (b + 1, s + LEAD - H)
                        if exists(bm):
                            if hm % GH == 0:
                                pe.wait_ge(stack_landed[hm // GH], (bm + 1) * (6 if causal else 3) * DMA)
                                if not causal and hm == 0:
                                    pe.wait_ge(ks_landed, (bm + 1) * 3 * DMA)
                            for qb in range(TB):
                                n = (bm * H + hm) * TB + qb
                                at(pe, m_reduced, n - 1)
                                w = (qb + 1) * P if causal else S
                                kr = ks[0:STACK, hm, 0:w] if causal else ks[0:STACK, par if bm is b else 1 - par, :]
                                pe.matmul(m_ps[:, qb % 2, 0:w], qs[0:STACK, hm, qb * P:(qb + 1) * P], kr,
                                          start=True, stop=True).then_inc(m_scored, 1)
                        if exists(b):
                            if j == 0:
                                pe.wait_ge(max_landed, (b * GROUPS + g + 1) * 2 * DMA)
                            done = [p[0] for p in parts]
                            for i, (bk, col, q0, kb) in enumerate(parts):
                                n = (b * H + s) * NE + bk
                                if bk not in done[:i]:
                                    at(pe, e_exped, n - NE + 1)
                                kr = ks[0:ROWS, s if causal else par, kb * P:(kb + 1) * P]
                                w = (S - q0) if causal else S
                                mm = pe.matmul(e_ps[:, bk, col:col + w], kr, qs[0:ROWS, s, q0:S], start=True, stop=True)
                                if bk not in done[i + 1:]:
                                    mm.then_inc(e_scored, 1)
                        bp, gp = (b, g - 1) if g else (b - 1, GROUPS - 1)
                        if exists(bp):
                            G = bp * GROUPS + gp
                            pp = par if bp is b else 1 - par
                            if j == 0:
                                if causal:
                                    pe.wait_ge(masked, (bp * H) + gp * GH + GH)
                                else:
                                    pe.wait_ge(e_exped, (bp * H + gp * GH + GH) * NE)
                                pe.wait_ge(v_evac, (bp + 1) * NV)
                                at(pe, o_evac, G)
                            kb = j
                            q0 = kb * P if causal else 0
                            c0 = start_of[kb]
                            for hh in range(GH):
                                head = gp * GH + hh if causal else 0
                                mm = pe.matmul(o_ps[32 * hh:32 * hh + 32, 0, q0:S], vo[:, pp, kb, head, :],
                                               probs[:, gp % 2, hh, c0:c0 + S - q0], start=kb == 0, stop=kb == TB - 1)
                            if j == GH - 1:
                                mm.then_inc(pv_done, 1)
                        if s in (4, 6) and exists(b + 1) and (s - 4) // 2 < NV:
                            i = (s - 4) // 2
                            pe.wait_ge(xt_split, (b + 2) * KC)
                            ps = bank("x0", (v_evac, (b + 1) * NV + i + 1))
                            for t in range(TB // NV):
                                for c in range(KC):
                                    tok = slice((i * (TB // NV) + t) * P, (i * (TB // NV) + t + 1) * P)
                                    mm = product(pe, ps[:, t * VC:(t + 1) * VC], [x[:, c, tok] for x in xt],
                                                 [w[:, c, :] for w in wv], c == 0, c == KC - 1)
                            mm.then_inc(v_made, 1)
                        if s in (8, 9) and exists(b + 2):
                            c = s - 8
                            pe.wait_ge(xn_landed, (b + 3) * DMA)
                            ps = bank("x0", (xt_split, (b + 2) * KC + c + 1))
                            for t in range(TB):
                                mm = pe.transpose(ps[:, t * P:(t + 1) * P], xn[:, t, c * P:(c + 1) * P], ident[:])
                            mm.then_inc(xt_turned, 1)
                        if 10 <= s < 10 + NQ and exists(b + 2):
                            i = s - 10
                            pe.wait_ge(xt_split, (b + 3) * KC)
                            ps = bank("x0", (qk_evac, (b + 2) * NQ + i + 1))
                            n = P if causal or i < 2 else HD
                            for c in range(KC):
                                mm = product(pe, ps[0:n, :], [w[:, c, i * P:i * P + n] for w in wqk],
                                             [x[:, c, :] for x in xt], c == 0, c == KC - 1)
                            mm.then_inc(qk_made, 1)
                        if s % GH == 1:
                            bt, gt = (b, g + 1) if g + 1 < GROUPS else (b + 1, 0)
                            if exists(bt):
                                pe.wait_ge(m_reduced, (bt * H + gt * GH + GH) * TB)
                                ps = bank("x1", (mx_split, bt * GROUPS + gt + 1))
                                pe.transpose(ps[0:GH * TB, 0:P], mx[:, gt * GH * TB:(gt + 1) * GH * TB],
                                             ident[:]).then_inc(mx_turned, 1)
                        if s % GH == 2:
                            bt, gt = (b, g - 2) if g >= 2 else (b - 1, g + 2)
                            if exists(bt):
                                G = bt * GROUPS + gt
                                pe.wait_ge(o_evac, G + 1)
                                ps = bank("x1", (o_normed, G + 1))
                                for t in range(TB):
                                    mm = pe.transpose(ps[:, t * P:(t + 1) * P], osb[:, t * P:(t + 1) * P], ident[:])
                                mm.then_inc(o_turned, 1)
                        if s in (7, 8) and exists(b - 1):
                            c = s - 7
                            pe.wait_ge(o_normed, b * GROUPS)
                            ps = bank("x1", (on_split, (b - 1) * KC + c + 1))
                            for t in range(TB):
                                mm = pe.transpose(ps[:, t * P:(t + 1) * P], on[:, t, c * P:(c + 1) * P], ident[:])
                            mm.then_inc(on_turned, 1)
                        if s in (11, 12) and exists(b - 1):
                            i = s - 11
                            pe.wait_ge(on_split, b * KC)
                            ps = bank("x1", (y_evac, (b - 1) * 2 + i + 1))
                            for t in range(2):
                                for c in range(KC):
                                    tok = slice((2 * i + t) * P, (2 * i + t + 1) * P)
                                    mm = product(pe, ps[:, t * D:(t + 1) * D], [o[:, c, tok] for o in ot],
                                                 [w[:, c, :] for w in wo], c == 0, c == KC - 1)
                            mm.then_inc(y_made, 1)

                over_batches(pe, body, -2, (2, 14), NB)

            @block.scalar
            def _(act):
                def body(b, par=None):
                    for s in range(H):
                        g, j = divmod(s, GH)
                        if j == 0:
                            bt, gt = (b, g - 2) if g >= 2 else (b - 1, g + 2)
                            if exists(bt):
                                G = bt * GROUPS + gt
                                act.wait_ge(pv_done, G + 1)
                                at(act, o_turned, G)
                                act.activation(osb[:], o_ps[:, 0, :], ACT.Copy).then_inc(o_evac, 1)
                        if exists(b):
                            if j == 0:
                                at(act, pv_done, b * GROUPS + g - 1)
                            for c in range(NE):
                                act.wait_ge(e_scored, (b * H + s) * NE + c + 1)
                                act.activation(probs[:, g % 2, j, c * S:c * S + width[c]], e_ps[:, c, 0:width[c]],
                                               ACT.Exp, scale=SCALE).then_inc(e_exped, 1)
                        if s == 0 and exists(b + 1):
                            src = rot if causal else qf
                            if causal:
                                act.wait_ge(summed, (b + 1) * 2 + 1)
                            else:
                                act.wait_ge(qk_evac, (b + 1) * NQ + 2)
                            at(act, q_written, (b + 1) * DMA)
                            act.activation(q_parts[:, 0], src[:], ACT.Copy).then_inc(q_hi, 1)
                        if s == 2 and exists(b + 1):
                            if causal:
                                act.wait_ge(summed, (b + 1) * 2 + 2)
                                at(act, k_written, (b + 1) * DMA)
                                act.activation(k_parts[:, 0], rot[:], ACT.Copy).then_inc(k_hi, 1)
                            else:
                                act.wait_ge(qk_evac, (b + 2) * NQ)
                                at(act, ks_landed, (b + 1) * 3 * DMA)
                                act.activation(k_parts[:, 0], kf[:], ACT.Copy).then_inc(k_hi, 1)
                        if s in (8, 9) and exists(b + 2):
                            c = s - 8
                            act.wait_ge(xt_turned, (b + 2) * KC + c + 1)
                            at(act, v_made, (b + 2) * NV)
                            act.activation(xt[0][:, c, :], x0_ps[:, 0, :], ACT.Copy).then_inc(xt_hi, 1)
                        if s in (7, 8) and exists(b - 1):
                            c = s - 7
                            act.wait_ge(on_turned, (b - 1) * KC + c + 1)
                            at(act, y_made, (b - 1) * 2)
                            act.activation(ot[0][:, c, :], x1_ps[:, 0, :], ACT.Copy).then_inc(on_hi, 1)
                        if 10 <= s < 10 + NQ and exists(b + 2):
                            i = s - 10
                            act.wait_ge(qk_made, (b + 2) * NQ + i + 1)
                            if causal:
                                at(act, roped, ((b + 1) * 2 + i // 2 + 1) * 4)
                                dst, n = (qf, kf)[i // 2][:, i % 2, :], P
                            elif i < 2:
                                at(act, q_split, b + 2)
                                dst, n = qf[:, i, :], P
                            else:
                                at(act, k_split, b + 2)
                                dst, n = kf[:], HD
                            act.activation(dst, x0_ps[0:n, 0, :], ACT.Identity, bias=bqk[0:n, i:i + 1]).then_inc(qk_evac, 1)

                over_batches(act, body, -2, (2, 14), NB)

            @block.vector
            def _(dve):
                chain = Chain(dve, dve_order, 2 * (GROUPS * 3 + 2 * 3))

                def body(b, par=None):
                    par = b % 2 if isinstance(b, int) else par

                    def normalise(i):
                        dve.wait_ge(rstd_made, (b - 1) * 2 + i + 1)
                        at(dve, stored, (b - 1) * DMA)
                        for t in range(2):
                            n = 2 * i + t
                            ins = dve.tensor_scalar(yo[:, n, :], hb[:, i, t, :], mv[:, n, 0:1], rstd[:, n:n + 1],
                                                    ALU.subtract, ALU.mult)
                        ins.then_inc(y_normed, 1)

                    for s in range(H):
                        g, j = divmod(s, GH)
                        bm, hm = (b, s + LEAD) if s + LEAD < H else (b + 1, s + LEAD - H)
                        if exists(bm):
                            for qb in range(TB):
                                n = (bm * H + hm) * TB + qb
                                if causal:
                                    at(dve, m_reduced, n - 1)
                                    at_alone(dve, m_scored, n + 1, dve_passed)
                                else:
                                    dve.wait_ge(m_scored, n + 1)
                                w = (qb + 1) * P
                                col = mx[:, hm * TB + qb:hm * TB + qb + 1]
                                if causal:
                                    dve.tensor_tensor_reduce(junk[:, qb % 2, 0:w], m_ps[:, qb % 2, 0:w],
                                                             mask[:, 512 - w:512], 1.0, MASKED,
                                                             ALU.add, ALU.max, col).then_inc(m_reduced, 1)
                                else:
                                    dve.tensor_reduce(col, m_ps[:, qb % 2, :], AX.X, ALU.max).then_inc(m_reduced, 1)
                        if s in (4, 6) and exists(b + 1) and (s - 4) // 2 < NV:
                            i = (s - 4) // 2
                            n = TB // NV
                            dve.wait_ge(v_made, (b + 1) * NV + i + 1)
                            src = x0_ps[:, 0, 0:n * VC].rearrange("p (t h d) -> p t h d", t=n, d=HD)
                            dst = vo[:, 1 - par, i * n:(i + 1) * n, :, 0:HD]
                            bias = spread(bv[:], [[0, n], [HD, KVH], [1, HD]])
                            dve.tensor_tensor(dst, src, bias, ALU.add).then_inc(v_evac, 1)
                        if s in (8, 9) and exists(b + 2):
                            c = s - 8
                            dve.wait_ge(xt_hi, (b + 2) * KC + c + 1)
                            dve.tensor_tensor(xt[1][:, c, :], x0_ps[:, 0, :], xt[0][:, c, :],
                                              ALU.subtract).then_inc(xt_split, 1)
                        if s % GH == 1:
                            bt, gt = (b, g + 1) if g + 1 < GROUPS else (b + 1, 0)
                            if exists(bt):
                                G = bt * GROUPS + gt
                                dve.wait_ge(mx_turned, G + 1)
                                at(dve, max_landed, G * 2 * DMA)
                                mt = x1_ps[0:GH * TB, 0, 0:P]
                                chain.then(dve.tensor_copy(mh[:, 0, :], mt))
                                dve.tensor_tensor(mh[:, 1, :], mt, mh[:, 0, :], ALU.subtract).then_inc(mx_split, 1)
                        if s % GH == 2:
                            bt, gt = (b, g - 2) if g >= 2 else (b - 1, g + 2)
                            if exists(bt):
                                dve.wait_ge(o_turned, bt * GROUPS + gt + 1)
                                o4 = x1_ps[:, 0, :].rearrange("p (t h e) -> p t h e", t=TB, h=GH)
                                sums = o4[:, :, :, HD:HD + 1].rearrange("p t h e -> p t (h e)")
                                d4 = den[:, 0, :].rearrange("p (t h) -> p t h", t=TB)
                                chain.then(dve.tensor_scalar(d4, sums, SUM_EPS if causal else 0.0, None, ALU.add))
                                chain.then(dve.reciprocal(den[:, 1, :], den[:, 0, :]))
                                r = spread(den[:, 1, :], [[GH, TB], [1, GH], [0, HD]])
                                o = on[:, :, gt * GH * HD:(gt + 1) * GH * HD].rearrange("p t (h d) -> p t h d", d=HD)
                                dve.tensor_tensor(o, o4[:, :, :, 0:HD], r, ALU.mult).then_inc(o_normed, 1)
                        if s == 1 and exists(b + 1):
                            dve.wait_ge(q_hi, b + 2)
                            dve.tensor_tensor(q_parts[:, 1], (rot if causal else qf)[:], q_parts[:, 0],
                                              ALU.subtract).then_inc(q_split, 1)
                            if causal:
                                dve.wait_ge(q_split, b + 2)
                                dve.wait_ge(roped, ((b + 1) * 2 + 2) * 4)
                                dve.tensor_tensor(rot[:, 0, :], prods[:, 0, :], prods[:, 1, :], ALU.subtract)
                                dve.tensor_tensor(rot[:, 1, :], prods[:, 2, :], prods[:, 3, :], ALU.add).then_inc(summed, 1)
                        if s == 3 and exists(b + 1):
                            dve.wait_ge(k_hi, b + 2)
                            kp = k_parts
                            dve.tensor_tensor(kp[:, 1], (rot if causal else kf)[:], kp[:, 0],
                                              ALU.subtract).then_inc(k_split, 1)
                        if s == 14 and causal and exists(b + 2):
                            dve.wait_ge(roped, ((b + 2) * 2 + 1) * 4)
                            at(dve, k_split, b + 2)
                            dve.tensor_tensor(rot[:, 0, :], prods[:, 0, :], prods[:, 1, :], ALU.subtract)
                            dve.tensor_tensor(rot[:, 1, :], prods[:, 2, :], prods[:, 3, :], ALU.add).then_inc(summed, 1)
                        if s in (7, 8) and exists(b - 1):
                            c = s - 7
                            dve.wait_ge(on_hi, (b - 1) * KC + c + 1)
                            dve.tensor_tensor(ot[1][:, c, :], x1_ps[:, 0, :], ot[0][:, c, :],
                                              ALU.subtract).then_inc(on_split, 1)
                        if s in (11, 12) and exists(b - 1):
                            i = s - 11
                            dve.wait_ge(y_made, (b - 1) * 2 + i + 1)
                            dve.wait_ge(xr_biased, b)
                            src = x1_ps[:, 0, :].rearrange("p (t d) -> p t d", t=2)
                            dve.tensor_tensor(hb[:, i], src, xr[:, 2 * i:2 * i + 2, :], ALU.add).then_inc(y_evac, 1)
                            dve.wait_ge(y_evac, (b - 1) * 2 + i + 1)
                            dve.bn_stats(stats[:, 2 * i, :], hb[:, i, 0, :])
                            chain.then(dve.bn_stats(stats[:, 2 * i + 1, :], hb[:, i, 1, :]), dve_passed)
                            dve.bn_aggr(mv[:, 2 * i, :], stats[:, 2 * i, :])
                            chain.then(dve.bn_aggr(mv[:, 2 * i + 1, :], stats[:, 2 * i + 1, :]))
                            dve.tensor_scalar(veps[:, 2 * i:2 * i + 2],
                                              mv[:, 2 * i:2 * i + 2, 1:2].rearrange("p t e -> p (t e)"),
                                              LN_EPS, None, ALU.add).then_inc(var_made, 1)
                        if s in (12, 13) and exists(b - 1):
                            normalise(s - 12)

                chain.per_two = 2 * (GROUPS * 3 + 2 * 2)
                over_batches(dve, body, -2, (2, 14), NB, chain)

            @block.gpsimd
            def _(pool):
                def body(b, par=None):
                    for s in range(H):
                        g, j = divmod(s, GH)
                        if causal and exists(b):
                            at_alone(pool, e_exped, (b * H + s + 1) * NE, pool_passed)
                            for kbs, step in (((0, 1, 2), 512), ((3,), 0)):
                                starts = sorted(start_of[kb] for kb in range(TB))
                                first = 896 if len(kbs) == 1 else 0
                                dims = [[512, 3], [1, P]] if first == 0 else [[1, P]]
                                blk = spread(probs[:, g % 2, j, first:first + 1], dims)
                                pattern = [[0, 3], [1, P]] if first == 0 else [[1, P]]
                                ins = pool.affine_select(out=blk, in_=blk, pattern=pattern, compare_op=ALU.is_ge,
                                                         fill=0.0, base=0, channel_multiplier=-1)
                            ins.then_inc(masked, 1)
                        if causal:
                            for slot, which, ahead, part in ((12, 0, 2, 0), (13, 0, 2, 1), (15, 1, 2, 0), (0, 1, 1, 1)):
                                bt = b + ahead
                                if s == slot and exists(bt):
                                    src = (qf, kf)[which]
                                    if part == 0:
                                        pool.wait_ge(qk_evac, bt * NQ + 2 * which + 2)
                                        at(pool, summed, bt * 2 + which)
                                    for e in range(2):
                                        pool.tensor_tensor(prods[:, 2 * part + e, :], src[:, e, :],
                                                           cs[:, (e + part) % 2, :], ALU.mult).then_inc(roped, 1)
                        if s == 8 and exists(b - 1):
                            pool.wait_ge(xr_landed, b * DMA)
                            pool.tensor_tensor(xr[:], xr[:], spread(bo[:], [[0, TB], [1, D]]), ALU.add).then_inc(xr_biased, 1)
                        if s in (11, 12) and exists(b - 1):
                            i = s - 11
                            pool.wait_ge(var_made, (b - 1) * 2 + i + 1)
                            pool.tensor_tensor(rstd[:, 2 * i:2 * i + 2], veps[:, 2 * i:2 * i + 2], mhalf[:],
                                               ALU.pow).then_inc(rstd_made, 1)

                over_batches(pool, body, -2, (2, 14), NB)

            @block.sync
            def _(sp):
                def rows(x, b):
                    return x[bass.ds(b, 1)].rearrange("o (t p) d -> p (o t) d", p=P)

                def body(b, par=None):
                    par = b % 2 if isinstance(b, int) else par

                    for s in range(H):
                        g = s // GH
                        if s % GH == 1:
                            bt, gt = (b, g + 1) if g + 1 < GROUPS else (b + 1, 0)
                            if exists(bt):
                                sp.wait_ge(mx_split, bt * GROUPS + gt + 1)
                                for r in range(2):
                                    sp.dma_start(qs[STACK + r:STACK + r + 1, gt * GH:(gt + 1) * GH, :].bitcast(F32),
                                                 mh[:, r, :].bitcast(F32)).then_inc(max_landed, DMA)
                        if s == 1 and exists(b + 1):
                            sp.wait_ge(q_split, b + 2)
                            sp.dma_start(q_dram[bass.ds(b + 1, 1)].rearrange("o r (e i) h t -> (o i h) (r e) t", e=2),
                                         q_parts.rearrange("p r e t -> p (r e) t").bitcast(F32)).then_inc(q_written, DMA)
                        if s == 4 and exists(b + 1):
                            sp.wait_ge(k_split, b + 2)
                            if causal:
                                sp.dma_start(k_dram[bass.ds(b + 1, 1)].rearrange("o r (e i) h t -> (o i h) (r e) t", e=2),
                                             k_parts.rearrange("p r e t -> p (r e) t").bitcast(F32)).then_inc(k_written, DMA)
                                sp.wait_ge(k_written, (b + 2) * DMA)
                            else:
                                at(sp, e_scored, b * H * NE)
                                for n, r in enumerate((0, 1, 0)):
                                    sp.dma_start(ks[n * HD:(n + 1) * HD, 1 - par, :].bitcast(F32),
                                                 k_parts[:, r, :].bitcast(F32)).then_inc(ks_landed, DMA)
                            sp.wait_ge(q_written, (b + 2) * DMA)
                        if s in (4, 7, 11, 15) and exists(b + 1):
                            gt = (4, 7, 11, 15).index(s)
                            at(sp, e_scored, (b * H + gt * GH + GH) * NE)
                            hs = slice(gt * GH, (gt + 1) * GH)
                            for n, (rq, rk) in enumerate(((0, 0), (0, 1), (1, 0))):
                                for dram, stack, r in ((q_dram, qs, rq), (k_dram, ks, rk))[:2 if causal else 1]:
                                    sp.dma_start(stack[n * HD:(n + 1) * HD, hs, :].bitcast(F32),
                                                 dram[bass.ds(b + 1, 1), r, :, hs, :].rearrange("o d h t -> (o d) h t")
                                                 ).then_inc(stack_landed[gt], DMA)
                        if s == 4 and exists(b + 2):
                            at(sp, xt_turned, (b + 2) * KC)
                            sp.dma_start(xn[:], rows(x_in, b + 2)).then_inc(xn_landed, DMA)
                        if s == 5 and exists(b - 1):
                            at(sp, y_evac, (b - 1) * 2)
                            sp.dma_start(xr[:], rows(x_in, b - 1)).then_inc(xr_landed, DMA)
                        if s == 14 and exists(b - 1):
                            sp.wait_ge(y_normed, b * 2)
                            sp.dma_start(rows(x_out, b - 1), yo[:]).then_inc(stored, DMA)

                over_batches(sp, body, -2, (2, 14), NB)
                sp.wait_ge(stored, NB * DMA)


def expert_layer(nc, sems, passed, name, x_in, x_out, gate, up_w, down_w, E, TOP, plain, glu, ident_in):
    U = plain + glu
    scaled = TOP == 1
    kinds = ["plain"] * plain + ["glu"] * glu
    DC = [2] * plain + [1] * glu
    d_first = [sum(DC[:u]) for u in range(U)]
    PAD = 8
    with ExitStack() as ctx:
        def sb(n, shape, dt=F32):
            return ctx.enter_context(nc.sbuf_tensor(f"{name}_{n}", shape, dt))

        def sem(n):
            return sems.enter_context(nc.semaphore(f"{name}_{n}"))

        w1 = [sb(f"w_up_{p}", [P, U, KC, 2 * P], F32R) for p in ("hi", "lo")]
        w2 = [sb(f"w_down_{p}", [P, sum(DC), D], F32R) for p in ("hi", "lo")]
        wg = [sb(f"w_gate_{p}", [P, KC, E], F32R) for p in ("hi", "lo")]
        xn = sb("x", [P, TB, D])
        xt = [sb(f"xT_{p}", [P, KC, S], F32R) for p in ("hi", "lo")]
        hf = sb("h", [P, 2 * S])
        ht = [sb(f"hT_{p}", [P, 2, 2 * S], F32R) for p in ("hi", "lo")]
        acc = sb("acc", [P, TB, D])
        yo = sb("y_out", [P, TB, D])
        ident = sb("identity", [P, P])
        lg = sb("logits", [P, TB, E + PAD])
        left = sb("logits_left", [P, TB, E + PAD])
        top8 = sb("top8", [P, TB, 8])
        top = sb("to_replace", [P, TB, 8])
        low = sb("shifted", [P, TB, E])
        ex = sb("exps", [P, TB, E])
        wt2 = sb("weights", [P, 2, TB, E])
        tot = sb("totals", [P, 2, TB])
        stats = sb("stats", [P, TB, 6])
        mv = sb("mean_var", [P, TB, 2])
        veps = sb("var_eps", [P, TB])
        rstd = sb("rstd", [P, TB])
        mhalf = sb("minus_half", [P, TB])
        xs = sb("x_scaled", [P, TB, D]) if scaled else xn

        def psum(n, banks):
            return ctx.enter_context(nc.psum_tensor(f"{name}_{n}", [P, banks, S], F32))

        h_ps = [psum("ps_h0", 2), psum("ps_h1", 2)]
        y_ps = psum("ps_y", 2)
        t_ps = psum("ps_turn", 2)

        const_landed, const_made = sem("const_landed"), sem("const_made")
        x_landed, stored = sem("x_landed"), sem("stored")
        x_turned, xt_hi, xt_split = sem("x_turned"), sem("xt_hi"), sem("xt_split")
        routed, logits_read, shifted, exped, weighed, x_scaled = (
            sem("routed"), sem("logits_read"), sem("shifted"), sem("exped"), sem("weighed"), sem("x_scaled"))
        h_made, h_silu, h_whole, h_hi, h_split = (
            sem("h_made"), sem("h_silu"), sem("h_whole"), sem("h_hi"), sem("h_split"))
        y_made, y_added, var_made, rstd_made, y_normed = (
            sem("y_made"), sem("y_added"), sem("var_made"), sem("rstd_made"), sem("y_normed"))
        dve_order = sem("dve_order")
        dve_passed, pool_passed = passed

        turns = 2 * KC if scaled else KC

        stage = sb("stage", [P, 2 * 512])
        specs = [(gate, *[w.rearrange("p c n -> p (c n)") for w in wg])]
        for u in range(U):
            specs.append((up_w[u], *[w[:, u].rearrange("p c n -> p (c n)") for w in w1]))
            specs.append((down_w[:, d_first[u]:d_first[u] + DC[u], :].rearrange("p c n -> p (c n)"),
                          *[w[:, d_first[u]:d_first[u] + DC[u], :].rearrange("p c n -> p (c n)") for w in w2]))
        load_split_weights(nc, sems, specs, stage, name)

        with nc.Block() as block:
            @block.sync
            def _(sp):
                sp.dma_start(ident[:], ident_in).then_inc(const_landed, DMA)
                sp.wait_ge(const_landed, DMA)

            @block.gpsimd
            def _(pool):
                pool.memset(mhalf[:], -0.5)
                pool.memset(lg[:], MASKED)

            @block.vector
            def _(dve):
                dve.memset(top[:], MASKED)

        def unit(b, u):
            return b * U + u

        with nc.Block() as block:
            @block.tensor
            def _(pe):
                def turn(b, n, src):
                    at(pe, xt_split, b * turns + n - 1)
                    for t in range(TB):
                        mm = pe.transpose(t_ps[:, n % 2, t * P:(t + 1) * P], src[:, t, (n % KC) * P:(n % KC + 1) * P],
                                          ident[:])
                    mm.then_inc(x_turned, 1)

                def route(b):
                    pe.wait_ge(xt_split, b * turns + KC)
                    for t in range(TB):
                        for c in range(KC):
                            mm = product(pe, t_ps[:, 0, t * E:(t + 1) * E], [x[:, c, t * P:(t + 1) * P] for x in xt],
                                         [w[:, c, :] for w in wg], c == 0, c == KC - 1)
                    mm.then_inc(routed, 1)

                def prepare(b):
                    pe.wait_ge(x_landed, (b + 1) * DMA)
                    at(pe, logits_read, b)
                    for c in range(KC):
                        turn(b, c, xn)
                    route(b)
                    if scaled:
                        pe.wait_ge(x_scaled, b + 1)
                        for c in range(KC):
                            if c == 0:
                                pe.wait_ge(logits_read, b + 1)
                            turn(b, KC + c, xs)

                def up(b, u):
                    n = unit(b, u)
                    if u == 0:
                        pe.wait_ge(xt_split, (b + 1) * turns)
                    at(pe, h_split, n - 1)
                    for m in range(2):
                        for c in range(KC):
                            mm = product(pe, h_ps[u % 2][:, m, :], [w[:, u, c, m * P:(m + 1) * P] for w in w1],
                                         [x[:, c, :] for x in xt], c == 0, c == KC - 1)
                    mm.then_inc(h_made, 1)

                def down(b, u):
                    n = unit(b, u)
                    pe.wait_ge(h_split, n + 1)
                    for i in range(2):
                        at(pe, y_added, 2 * n + i - 1)
                        for t in range(2):
                            tok = (2 * i + t) * P
                            for c in range(DC[u]):
                                mm = product(pe, y_ps[:, i, t * D:(t + 1) * D],
                                             [h[:, u % 2, c * S + tok:c * S + tok + P] for h in ht],
                                             [w[:, d_first[u] + c, :] for w in w2], c == 0, c == DC[u] - 1)
                        mm.then_inc(y_made, 1)

                def body(b, par=None):
                    if exists(b):
                        for u in range(U):
                            up(b, u)
                            if u == U - 1 and exists(b + 1):
                                prepare(b + 1)
                            if u or exists(b - 1):
                                down(*((b, u - 1) if u else (b - 1, U - 1)))
                    elif b < 0:
                        prepare(0)
                    else:
                        down(b - 1, U - 1)

                over_batches(pe, body, -1, (2, 14), NB)

            @block.scalar
            def _(act):
                def prepare(b):
                    for n in range(turns):
                        act.wait_ge(x_turned, b * turns + n + 1)
                        if n == 0:
                            at(act, h_made, unit(b, 0))
                        if n == KC:
                            act.wait_ge(routed, b + 1)
                        act.activation(xt[0][:, n % KC, :], t_ps[:, n % 2, :], ACT.Copy).then_inc(xt_hi, 1)
                        if n == KC - 1:
                            act.wait_ge(shifted, b + 1)
                            act.activation(ex[:, :, 0:E if TOP > 1 else 1], low[:, :, 0:E if TOP > 1 else 1],
                                           ACT.Exp).then_inc(exped, 1)

                def hidden(b, u):
                    n = unit(b, u)
                    act.wait_ge(h_made, n + 1)
                    w = 2 * S if kinds[u] == "plain" else S
                    at(act, h_split, n)
                    act.activation(hf[:, 0:w], h_ps[u % 2].rearrange("p m s -> p (m s)")[:, 0:w],
                                   ACT.Silu).then_inc(h_silu, 1)
                    if kinds[u] == "glu":
                        act.wait_ge(h_whole, b * glu + (u - plain) + 1)
                    else:
                        act.wait_ge(h_silu, n + 1)
                    at(act, y_made, 2 * (n - 1))
                    act.activation(ht[0][:, u % 2, 0:w], hf[:, 0:w], ACT.Copy).then_inc(h_hi, 1)

                def body(b, par=None):
                    if exists(b):
                        for u in range(U):
                            hidden(b, u)
                            if u == U - 1 and exists(b + 1):
                                prepare(b + 1)
                    elif b < 0:
                        prepare(0)

                over_batches(act, body, -1, (2, 14), NB)

            @block.vector
            def _(dve):
                chain = Chain(dve, dve_order, 0)

                def lo_part(b, n):
                    dve.wait_ge(xt_hi, b * turns + n + 1)
                    dve.tensor_tensor(xt[1][:, n % KC, :], t_ps[:, n % 2, :], xt[0][:, n % KC, :],
                                      ALU.subtract).then_inc(xt_split, 1)

                def prepare(b, par):
                    wt = wt2[:, par]
                    for n in range(KC):
                        lo_part(b, n)
                    dve.wait_ge(routed, b + 1)
                    dve.tensor_copy(lg[:, :, 0:E], t_ps[:, 0, 0:TB * E].rearrange("p (t e) -> p t e", t=TB)
                                    ).then_inc(logits_read, 1)
                    at_alone(dve, logits_read, b + 1, dve_passed)
                    for t in range(TB):
                        ins = dve.max(top8[:, t, :], lg[:, t, 0:E])
                    chain.then(ins)
                    chain.then(dve.tensor_copy(top[:, :, 0:TOP], top8[:, :, 0:TOP]), dve_passed)
                    for t in range(TB):
                        ins = dve.match_replace(left[:, t, :], top[:, t, :], lg[:, t, :], -3.3e38)
                    chain.then(ins)
                    if TOP > 1:
                        biggest = spread(top8[:], [[8, TB], [0, E]])
                        dve.tensor_tensor(low[:], lg[:, :, 0:E], biggest, ALU.subtract).then_inc(shifted, 1)
                        chain.then(dve.tensor_tensor(wt, left[:, :, 0:E], lg[:, :, 0:E], ALU.not_equal))
                        dve.wait_ge(exped, b + 1)
                        chain.then(dve.tensor_tensor(wt, wt, ex[:], ALU.mult))
                        chain.then(dve.tensor_reduce(tot[:, 0, :], wt, AX.X, ALU.add))
                        chain.then(dve.reciprocal(tot[:, 1, :], tot[:, 0, :]))
                        dve.tensor_tensor(wt, wt, spread(tot[:, 1, :], [[1, TB], [0, E]]),
                                          ALU.mult).then_inc(weighed, 1)
                    else:
                        dve.tensor_scalar(low[:, :, 0:1], top8[:, :, 0:1], -1.0, None, ALU.mult).then_inc(shifted, 1)
                        dve.tensor_tensor(wt, left[:, :, 0:E], lg[:, :, 0:E], ALU.not_equal).then_inc(weighed, 1)
                        dve.wait_ge(exped, b + 1)
                        chain.then(dve.tensor_scalar(tot[:, 0, :], ex[:, :, 0:1].rearrange("p t e -> p (t e)"),
                                                     1.0, None, ALU.add))
                        chain.then(dve.reciprocal(tot[:, 1, :], tot[:, 0, :]))
                        for t in range(TB):
                            ins = dve.tensor_scalar(xs[:, t, :], xn[:, t, :], tot[:, 1, t:t + 1], None, ALU.mult)
                        ins.then_inc(x_scaled, 1)
                        for n in range(KC, turns):
                            lo_part(b, n)

                def hidden(b, u):
                    n = unit(b, u)
                    w = 2 * S if kinds[u] == "plain" else S
                    if kinds[u] == "glu":
                        dve.wait_ge(h_silu, n + 1)
                        dve.tensor_tensor(hf[:, 0:S], hf[:, 0:S], h_ps[u % 2][:, 1, :], ALU.mult).then_inc(h_whole, 1)
                    dve.wait_ge(h_hi, n + 1)
                    dve.tensor_tensor(ht[1][:, u % 2, 0:w], hf[:, 0:w], ht[0][:, u % 2, 0:w],
                                      ALU.subtract).then_inc(h_split, 1)

                def add_up(b, u, par):
                    n = unit(b, u)
                    if u == 0:
                        dve.wait_ge(weighed, b + 1)
                    else:
                        dve.wait_ge(y_added, 2 * n)
                    for i in range(2):
                        dve.wait_ge(y_made, 2 * n + i + 1)
                        for t in range(2):
                            k = 2 * i + t
                            weight = wt2[:, par, k, u:u + 1] if u < E else 1.0
                            ins = dve.scalar_tensor_tensor(out=acc[:, k, :], in0=y_ps[:, i, t * D:(t + 1) * D],
                                                           scalar=weight, in1=(acc if u else xn)[:, k, :],
                                                           op0=ALU.mult, op1=ALU.add)
                        ins.then_inc(y_added, 1)

                def moments(b):
                    dve.wait_ge(y_added, (b + 1) * U * 2)
                    for t in range(TB):
                        ins = dve.bn_stats(stats[:, t, :], acc[:, t, :])
                    chain.then(ins, dve_passed)
                    for t in range(TB):
                        ins = dve.bn_aggr(mv[:, t, :], stats[:, t, :])
                    chain.then(ins)
                    dve.tensor_scalar(veps[:], mv[:, :, 1:2].rearrange("p t e -> p (t e)"), LN_EPS, None,
                                      ALU.add).then_inc(var_made, 1)

                def normalise(b):
                    dve.wait_ge(rstd_made, b + 1)
                    at(dve, stored, b * DMA)
                    for t in range(TB):
                        ins = dve.tensor_scalar(yo[:, t, :], acc[:, t, :], mv[:, t, 0:1], rstd[:, t:t + 1],
                                                ALU.subtract, ALU.mult)
                    ins.then_inc(y_normed, 1)
                    dve.wait_ge(y_normed, b + 1)

                def body(b, par=None):
                    par = b % 2 if isinstance(b, int) else par
                    if exists(b):
                        for u in range(U):
                            hidden(b, u)
                            if u == U - 1 and exists(b + 1):
                                prepare(b + 1, 1 - par)
                            if u == 1 and exists(b - 1):
                                normalise(b - 1)
                            if u:
                                add_up(b, u - 1, par)
                            elif exists(b - 1):
                                add_up(b - 1, U - 1, 1 - par)
                                moments(b - 1)
                    elif b < 0:
                        prepare(0, 0)
                    else:
                        add_up(b - 1, U - 1, 1 - par)
                        moments(b - 1)
                        normalise(b - 1)

                chain.per_two = 2 * ((7 if TOP > 1 else 5) + 2)
                over_batches(dve, body, -1, (2, 14), NB, chain)

            @block.gpsimd
            def _(pool):
                def body(b, par=None):
                    if exists(b - 1):
                        pool.wait_ge(var_made, b)
                        pool.tensor_tensor(rstd[:], veps[:], mhalf[:], ALU.pow).then_inc(rstd_made, 1)

                over_batches(pool, body, -1, (2, 14), NB)

            @block.sync
            def _(sp):
                def rows(x, b):
                    return x[bass.ds(b, 1)].rearrange("o (t p) d -> p (o t) d", p=P)

                def body(b, par=None):
                    if exists(b + 1):
                        at(sp, y_added, unit(b, 0) * 2 + 2)
                        sp.dma_start(xn[:], rows(x_in, b + 1)).then_inc(x_landed, DMA)
                    if exists(b - 1):
                        sp.wait_ge(y_normed, b)
                        sp.dma_start(rows(x_out, b - 1), yo[:]).then_inc(stored, DMA)

                over_batches(sp, body, -1, (2, 14), NB)
                sp.wait_ge(stored, NB * DMA)


def phase(nc, sems, passed, which, x, out, a):
    if which == "a0":
        attention_layer(nc, sems, passed, "l0", True, x, out, (a["l0_wqk"], a["l0_wv"]), (a["l0_bqk"], a["l0_bv"]),
                        a["l0_wo"], a["l0_bo"], (a["cos_sin"],), a["ident"])
    if which == "e0":
        expert_layer(nc, sems, passed, "e0", x, out, a["e0_gate"], a["e0_up"], a["e0_down"], 16, 4, 16, 2, a["ident"])
    if which == "a1":
        attention_layer(nc, sems, passed, "l1", False, x, out, (a["l1_wqk"], a["l1_wv"]), (a["l1_bqk"], a["l1_bv"]),
                        a["l1_wo"], a["l1_bo"], (), a["ident"])
    if which == "e1":
        expert_layer(nc, sems, passed, "e1", x, out, a["e1_gate"], a["e1_up"], a["e1_down"], 8, 1, 0, 8, a["ident"])


def program(nc, x, out, a):
    between = [nc.dram_tensor(n, [NB, S, D], F32, kind="Internal").ap() for n in ("x1", "x2", "x3")]
    stops = [x, *between, out]
    with ExitStack() as sems:
        passed = [sems.enter_context(nc.semaphore(n)) for n in ("dve_passed", "pool_passed")]
        for n, which in enumerate(("a0", "e0", "a1", "e1")):
            phase(nc, sems, passed, which, stops[n], stops[n + 1], a)


def layouts(i):
    f = {k: np.asarray(v) for k, v in i.items()}

    def chunks(w):
        return np.ascontiguousarray(w.reshape(KC, P, -1).transpose(1, 0, 2).reshape(P, -1))

    def rowwise(v, n=P):
        return np.ascontiguousarray(np.broadcast_to(v.reshape(1, -1), (n, v.size)))

    order = np.arange(D).reshape(H, HALF, 2).transpose(2, 1, 0).reshape(-1)
    one_head = np.arange(HD).reshape(HALF, 2).T.reshape(-1)
    wt = f["L0_attn_w_qkv"].T
    bq = f["L0_attn_b_qkv"]
    a = {
        "l0_wqk": chunks(np.concatenate([wt[:, :D][:, order], wt[:, D:2 * D][:, order]], 1)),
        "l0_wv": chunks(wt[:, 2 * D:]),
        "l0_bqk": np.ascontiguousarray(np.concatenate([bq[:D][order], bq[D:2 * D][order]]).reshape(4, P).T),
        "l0_bv": rowwise(bq[2 * D:]),
        "l0_wo": chunks(f["L0_attn_w_out"].T),
        "l0_bo": rowwise(f["L0_attn_b_out"]),
    }
    a["l1_wqk"] = chunks(np.concatenate([f["L1_attn_Wq"][:, order], f["L1_attn_Wk"][:, one_head]], 1))
    a["l1_wv"] = chunks(f["L1_attn_Wv"])
    pad = np.zeros(P - HD, np.float32)
    a["l1_bqk"] = np.ascontiguousarray(np.concatenate([f["L1_attn_bq"][order], f["L1_attn_bk"][one_head], pad]).reshape(3, P).T)
    a["l1_bv"] = rowwise(f["L1_attn_bv"])
    a["l1_wo"] = chunks(f["L1_attn_Wo"])
    a["l1_bo"] = rowwise(f["L1_attn_bo"])
    gu = f["L0_ffn_shared_gu"].T
    shared = [np.concatenate([gu[:, u * P:(u + 1) * P], gu[:, D + u * P:D + (u + 1) * P]], 1) for u in range(2)]
    a["e0_gate"] = chunks(f["L0_ffn_gate_w"].T)
    a["e0_up"] = np.stack([chunks(w.T) for w in f["L0_ffn_w1"]] + [chunks(w) for w in shared])
    down = np.concatenate([w.T for w in f["L0_ffn_w2"]] + [f["L0_ffn_shared_down"].T], 0)
    a["e0_down"] = np.ascontiguousarray(down.reshape(-1, P, D).transpose(1, 0, 2))
    a["e1_gate"] = chunks(f["L1_ffn_gate_w"].T)
    a["e1_up"] = np.stack([chunks(np.concatenate([g.T, u.T], 1)) for g, u in zip(f["L1_ffn_w_gate"], f["L1_ffn_w_up"])])
    a["e1_down"] = np.ascontiguousarray(f["L1_ffn_w_down"].transpose(2, 0, 1))
    inv = (10000.0 ** (-np.arange(0, HD, 2, dtype=np.float32) / HD)).astype(np.float32)
    ang = np.arange(S, dtype=np.float32)[None, :] * inv[:, None]
    a["cos_sin"] = np.repeat(np.stack([np.cos(ang), np.sin(ang)], 1), H, 0).astype(np.float32)
    a["ident"] = np.eye(P, dtype=np.float32)
    return a


def kernel(**inputs):
    import concourse.bacc as bacc
    from concourse.bass_utils import run_bass_kernel_spmd

    nc = bacc.Bacc("TRN2", target_bir_lowering=False, num_devices=1, dynamic_dma_scratch_size=64)
    arrays = {"x": np.ascontiguousarray(inputs["L0_attn_x"]), **layouts(inputs)}
    aps = {n: nc.dram_tensor(n, list(v.shape), F32, kind="ExternalInput").ap() for n, v in arrays.items()}
    out = nc.dram_tensor("out", [NB, S, D], F32, kind="ExternalOutput").ap()
    program(nc, aps.pop("x"), out, aps)
    r = run_bass_kernel_spmd(nc, [arrays], core_ids=[0])
    return r.results[0]["out"]
```

```python
from contextlib import ExitStack

import numpy as np

import concourse.bass as bass
from concourse import mybir

F32, F32R, BF16 = mybir.dt.float32, mybir.dt.float32r, mybir.dt.bfloat16
ALU, ACT, AX = mybir.AluOpType, mybir.ActivationFunctionType, mybir.AxisListType

P = 128
NB, S, D = 16, 512, 256
H, HD = 16, 16
TB = S // P
KC = D // P
HALF = HD // 2
GROUPS, GH = 4, 4
SPLITS = 3
STACK = SPLITS * HD
MAX_ROW = P - 2
LEAD = 7
SCALE = 1.0 / float(np.sqrt(HD))
LN_EPS, SUM_EPS = 1e-5, 1e-8
MASKED = -3.0e38
DMA = 16


def at(eng, sem, value):
    if not isinstance(value, int) or value > 0:
        eng.wait_ge(sem, value)


def at_most(value, most):
    return min(value, most) if isinstance(value, int) else value


def at_alone(eng, sem, value, passed):
    at(eng, sem, value)
    if not isinstance(value, int):
        eng.sem_inc(passed, 1)


class Chain:

    def __init__(self, eng, sem, per_two):
        self.eng, self.sem, self.n, self.per_two = eng, sem, 0, per_two

    def then(self, instruction, alone=None):
        self.n = self.n + 1
        instruction.then_inc(self.sem, 1)
        if alone:
            at_alone(self.eng, self.sem, self.n, alone)
        else:
            self.eng.wait_ge(self.sem, self.n)


def over_batches(eng, body, first, looped, last, chain=None):
    lo, hi = looped
    for b in range(first, lo):
        body(b)
    before = chain.n if chain else 0
    with eng.Fori(0, (hi - lo) // 2) as i:
        if chain:
            chain.n = i * chain.per_two + before
        body(i * 2 + lo, 0)
        body(i * 2 + (lo + 1), 1)
    if chain:
        chain.n = before + (hi - lo) // 2 * chain.per_two
    for b in range(hi, last + 1):
        body(b)


def exists(b):
    return not isinstance(b, int) or 0 <= b < NB


def spread(ap, dims):
    return bass.AP(ap.tensor, ap.offset, [list(ap.ap[0])] + dims)


def product(pe, out, a, b, start=True, stop=True):
    pe.matmul(out, a[0], b[0], start=start, stop=False)
    pe.matmul(out, a[1], b[0], start=False, stop=False)
    return pe.matmul(out, a[0], b[1], start=False, stop=stop)


def load_split_weights(nc, sems, specs, stage, name):
    landed = sems.enter_context(nc.semaphore(f"{name}_weights_landed"))
    hi_done = sems.enter_context(nc.semaphore(f"{name}_weights_hi"))
    lo_done = sems.enter_context(nc.semaphore(f"{name}_weights_lo"))
    half = stage.shape[1] // 2

    def staged(n, w):
        return stage[: w, (n % 2) * half:(n % 2) * half + size(n)]

    def size(n):
        return int(np.prod(specs[n][0].shape[1:]))

    with nc.Block() as block:
        @block.sync
        def _(sp):
            for n, (src, hi, lo) in enumerate(specs):
                at(sp, lo_done, n - 1)
                sp.dma_start(staged(n, src.shape[0]), src).then_inc(landed, DMA)
                sp.wait_ge(landed, DMA * (n + 1))

        @block.scalar
        def _(act):
            for n, (src, hi, lo) in enumerate(specs):
                act.wait_ge(landed, DMA * (n + 1))
                act.activation(hi, staged(n, src.shape[0]), ACT.Copy).then_inc(hi_done, 1)

        @block.vector
        def _(dve):
            for n, (src, hi, lo) in enumerate(specs):
                dve.wait_ge(hi_done, n + 1)
                dve.tensor_tensor(lo, staged(n, src.shape[0]), hi, ALU.subtract).then_inc(lo_done, 1)


def attention_layer(nc, sems, passed, name, causal, x_in, x_out, w_qkv, b_qkv, w_out, b_out, tables, ident_in):
    NQ = 4 if causal else 3
    NV = 2 if causal else 1
    NE = 3 if causal else 4
    PW = 1280 if causal else TB * S
    KVH = H if causal else 1
    parts = [(0, 0, 0, 0), (1, 0, 128, 1), (1, 384, 384, 3), (2, 0, 256, 2)] if causal else [
        (kb, 0, 0, kb) for kb in range(TB)]
    start_of = {kb: bank * S + col for bank, col, q0, kb in parts}
    width = {0: S, 1: S, 2: 256} if causal else {kb: S for kb in range(TB)}
    VC = D if causal else HD
    E_BANKS = 3

    def e_bank(head, part):
        return (head * NE + part) % E_BANKS

    with ExitStack() as ctx:
        def sb(n, shape, dt=F32):
            return ctx.enter_context(nc.sbuf_tensor(f"{name}_{n}", shape, dt))

        def sem(n):
            return sems.enter_context(nc.semaphore(f"{name}_{n}"))

        q_dram = nc.dram_tensor(f"{name}_q_stacked", [NB, 2, HD, H, S], F32, kind="Internal").ap()
        k_dram = nc.dram_tensor(f"{name}_k_stacked", [NB, 2, HD, H, S], F32, kind="Internal").ap() if causal else None

        qs = sb("q_stack", [P, H, S], F32R)
        ks = sb("k_stack", [P, H if causal else 2, S], F32R)
        probs = sb("probs", [P, 2, GH, PW])
        vo = sb("v_ones", [P, 2, TB, KVH, 32])
        xn = sb("x_to_turn", [P, TB, D])
        xr = sb("x_residual", [P, TB, D])
        xt = [sb(f"xT_{p}", [P, KC, S], F32R) for p in ("hi", "lo")]
        qf = sb("q_projected", [P, 2, S])
        kf = sb("k_projected", [P, 2, S]) if causal else sb("k_projected", [HD, S])
        q_parts = sb("q_parts", [P, 2, 2, S], F32R)
        k_parts = sb("k_parts", [P, 2, 2, S], F32R) if causal else sb("k_parts", [HD, 2, S], F32R)
        mx = sb("row_max", [P, H * TB])
        mh = sb("max_parts", [GH * TB, 2, P], F32R)
        osb = sb("o_raw", [P, S])
        on = sb("o_normed", [P, TB, D])
        ot = [sb(f"oT_{p}", [P, KC, S], F32R) for p in ("hi", "lo")]
        den = sb("denominators", [P, 2, GH * TB])
        hb = sb("h", [P, 2, 2, D])
        stats = sb("stats", [P, 4, 6])
        mv = sb("mean_var", [P, 4, 2])
        veps = sb("var_eps", [P, 4])
        rstd = sb("rstd", [P, 4])
        mhalf = sb("minus_half", [P, 2])
        yo = sb("y_out", [P, TB, D])
        bo = sb("b_out", [P, D])
        ident = sb("identity", [P, P])
        QKC = 2 * D if causal else D + HD
        wqk = [sb(f"w_qk_{p}", [P, KC, QKC], F32R) for p in ("hi", "lo")]
        wv = [sb(f"w_v_{p}", [P, KC, VC], F32R) for p in ("hi", "lo")]
        wo = [sb(f"w_o_{p}", [P, KC, D], F32R) for p in ("hi", "lo")]
        bqk = sb("b_qk", [P, NQ])
        bv = sb("b_v", [P, VC])
        if causal:
            prods = sb("rope_products", [P, 4, S])
            rot = sb("rope_sums", [P, 2, S])
            cs = sb("cos_sin", [P, 2, S])
            mask = sb("causal_mask", [P, S], BF16)
            junk = sb("junk", [P, 2, S], BF16)

        def psum(n, banks):
            return ctx.enter_context(nc.psum_tensor(f"{name}_{n}", [P, banks, S], F32))

        m_ps = psum("ps_max", 2)
        e_ps = psum("ps_exp", E_BANKS)
        o_ps = psum("ps_o", 1)
        x0_ps = psum("ps_x0", 1)
        x1_ps = psum("ps_x1", 1)

        const_landed, const_made = sem("const_landed"), sem("const_made")
        xn_landed, xr_landed, xr_biased = sem("xn_landed"), sem("xr_landed"), sem("xr_biased")
        q_written, k_written, max_landed = sem("q_written"), sem("k_written"), sem("max_landed")
        stack_landed = [sem(f"stack_landed_{g}") for g in range(GROUPS)]
        ks_landed, stored = sem("ks_landed"), sem("stored")
        m_scored, m_reduced, e_scored, e_exped, masked = (
            sem("m_scored"), sem("m_reduced"), sem("e_scored"), sem("e_exped"), sem("masked"))
        pv_done, o_evac, o_turned, o_normed = sem("pv_done"), sem("o_evac"), sem("o_turned"), sem("o_normed")
        mx_turned, mx_split = sem("mx_turned"), sem("mx_split")
        xt_turned, xt_hi, xt_split = sem("xt_turned"), sem("xt_hi"), sem("xt_split")
        qk_made, qk_evac, v_made, v_evac = sem("qk_made"), sem("qk_evac"), sem("v_made"), sem("v_evac")
        roped, summed = sem("roped"), sem("summed")
        q_hi, q_split, k_hi, k_split = sem("q_hi"), sem("q_split"), sem("k_hi"), sem("k_split")
        on_turned, on_hi, on_split = sem("on_turned"), sem("on_hi"), sem("on_split")
        y_made, y_evac, var_made, rstd_made, y_normed = (
            sem("y_made"), sem("y_evac"), sem("var_made"), sem("rstd_made"), sem("y_normed"))
        dve_order = sem("dve_order")
        dve_passed, pool_passed = passed

        stage = probs.rearrange("p a b c -> p (a b c)")[:, 0:4096]
        load_split_weights(nc, sems, [
            (w_qkv[0], *[w.rearrange("p c n -> p (c n)") for w in wqk]),
            (w_qkv[1], *[w.rearrange("p c n -> p (c n)") for w in wv]),
            (w_out, *[w.rearrange("p c n -> p (c n)") for w in wo]),
        ], stage, name)

        with nc.Block() as block:
            @block.sync
            def _(sp):
                loads = [(ident[:], ident_in), (bqk[:], b_qkv[0]), (bv[:], b_qkv[1]), (bo[:], b_out)]
                if causal:
                    loads += [(cs[:], tables[0])]
                for dst, src in loads:
                    sp.dma_start(dst, src).then_inc(const_landed, DMA)
                sp.wait_ge(const_landed, DMA * len(loads))

            @block.gpsimd
            def _(pool):
                pool.memset(mhalf[:], -0.5)
                pool.memset(vo[:], 0.0).then_inc(const_made, 1)
                pool.wait_ge(const_made, 1)
                pool.memset(vo[:, :, :, :, HD:HD + 1], 1.0)
                if causal:
                    pool.memset(mask[:], 0.0).then_inc(const_made, 1)
                    pool.wait_ge(const_made, 2)
                    pool.affine_select(out=mask[:], in_=mask[:], pattern=[[-1, S]], compare_op=ALU.is_ge,
                                       fill=MASKED, base=384, channel_multiplier=1)

            @block.vector
            def _(dve):
                dve.memset(ks[:].bitcast(F32), -1.0)
                dve.memset(qs[:].bitcast(F32), 0.0)

        def x_start(b):
            x0 = (qk_evac, at_most((b + 2) * NQ, NB * NQ))
            if isinstance(b, int) and b <= 0:
                return x0, (mx_split, b + 1)
            return x0, (o_normed, (b - 1) * GROUPS + 2)

        with nc.Block() as block:
            @block.tensor
            def _(pe):
                def body(b, par=None):
                    par = b % 2 if isinstance(b, int) else par
                    free = dict(zip(("x0", "x1"), x_start(b)))

                    def bank(which, emptied):
                        at(pe, *free[which])
                        free[which] = emptied
                        return (x1_ps if which == "x1" else x0_ps)[:, 0, :]

                    for s in range(H):
                        g, j = divmod(s, GH)
                        bm, hm = (b, s + LEAD) if s + LEAD < H else (b + 1, s + LEAD - H)

                        def row_scores(*blocks):
                            if not exists(bm):
                                return
                            if hm % GH == 0 and blocks[0] == 0:
                                pe.wait_ge(stack_landed[hm // GH], (bm + 1) * (6 if causal else 3) * DMA)
                                if not causal and hm == 0:
                                    pe.wait_ge(ks_landed, (bm + 1) * 3 * DMA)
                            for qb in blocks:
                                n = (bm * H + hm) * TB + qb
                                at(pe, m_reduced, n - 1)
                                w = (qb + 1) * P if causal else S
                                kr = ks[0:MAX_ROW, hm, 0:w] if causal else ks[0:MAX_ROW, par if bm is b else 1 - par, :]
                                pe.matmul(m_ps[:, qb % 2, 0:w], qs[0:MAX_ROW, hm, qb * P:(qb + 1) * P], kr,
                                          start=True, stop=True).then_inc(m_scored, 1)

                        row_scores(0)
                        if exists(b):
                            if j == 0:
                                pe.wait_ge(max_landed, (b * GROUPS + g + 1) * 2 * DMA)
                            done = [p[0] for p in parts]
                            for i, (bk, col, q0, kb) in enumerate(parts):
                                n = (b * H + s) * NE + bk
                                if bk not in done[:i]:
                                    at(pe, e_exped, n if s == 0 and bk == 0 and not causal else n - E_BANKS + 1)
                                kr = ks[:, s if causal else par, kb * P:(kb + 1) * P]
                                w = (S - q0) if causal else S
                                mm = pe.matmul(e_ps[:, e_bank(s, bk), col:col + w], kr, qs[:, s, q0:S], start=True, stop=True)
                                if bk not in done[i + 1:]:
                                    mm.then_inc(e_scored, 1)
                                if i == (0 if causal else 1):
                                    row_scores(1)
                        else:
                            row_scores(1)
                        row_scores(2)
                        bp, gp = (b, g - 1) if g else (b - 1, GROUPS - 1)
                        if exists(bp):
                            G = bp * GROUPS + gp
                            pp = par if bp is b else 1 - par
                            if j == 0:
                                if causal:
                                    pe.wait_ge(masked, (bp * H) + gp * GH + GH)
                                else:
                                    pe.wait_ge(e_exped, (bp * H + gp * GH + GH) * NE)
                                pe.wait_ge(v_evac, (bp + 1) * NV)
                                at(pe, o_evac, G)
                            kb = j
                            q0 = kb * P if causal else 0
                            c0 = start_of[kb]
                            for hh in range(GH):
                                head = gp * GH + hh if causal else 0
                                mm = pe.matmul(o_ps[32 * hh:32 * hh + 32, 0, q0:S], vo[:, pp, kb, head, :],
                                               probs[:, gp % 2, hh, c0:c0 + S - q0], start=kb == 0, stop=kb == TB - 1)
                            if j == GH - 1:
                                mm.then_inc(pv_done, 1)
                        row_scores(3)
                        if s in (4, 6) and exists(b + 1) and (s - 4) // 2 < NV:
                            i = (s - 4) // 2
                            pe.wait_ge(xt_split, (b + 2) * KC)
                            ps = bank("x0", (v_evac, (b + 1) * NV + i + 1))
                            for t in range(TB // NV):
                                for c in range(KC):
                                    tok = slice((i * (TB // NV) + t) * P, (i * (TB // NV) + t + 1) * P)
                                    mm = product(pe, ps[:, t * VC:(t + 1) * VC], [x[:, c, tok] for x in xt],
                                                 [w[:, c, :] for w in wv], c == 0, c == KC - 1)
                            mm.then_inc(v_made, 1)
                        if s in (8, 9) and exists(b + 2):
                            c = s - 8
                            pe.wait_ge(xn_landed, (b + 3) * DMA)
                            ps = bank("x0", (xt_split, (b + 2) * KC + c + 1))
                            for t in range(TB):
                                mm = pe.transpose(ps[:, t * P:(t + 1) * P], xn[:, t, c * P:(c + 1) * P], ident[:])
                            mm.then_inc(xt_turned, 1)
                        if 10 <= s < 10 + NQ and exists(b + 2):
                            i = s - 10
                            pe.wait_ge(xt_split, (b + 3) * KC)
                            ps = bank("x0", (qk_evac, (b + 2) * NQ + i + 1))
                            n = P if causal or i < 2 else HD
                            for c in range(KC):
                                mm = product(pe, ps[0:n, :], [w[:, c, i * P:i * P + n] for w in wqk],
                                             [x[:, c, :] for x in xt], c == 0, c == KC - 1)
                            mm.then_inc(qk_made, 1)
                        if s % GH == 1:
                            bt, gt = (b, g + 1) if g + 1 < GROUPS else (b + 1, 0)
                            if exists(bt):
                                pe.wait_ge(m_reduced, (bt * H + gt * GH + GH) * TB)
                                ps = bank("x1", (mx_split, bt * GROUPS + gt + 1))
                                pe.transpose(ps[0:GH * TB, 0:P], mx[:, gt * GH * TB:(gt + 1) * GH * TB],
                                             ident[:]).then_inc(mx_turned, 1)
                        if s % GH == 2:
                            bt, gt = (b, g - 2) if g >= 2 else (b - 1, g + 2)
                            if exists(bt):
                                G = bt * GROUPS + gt
                                pe.wait_ge(o_evac, G + 1)
                                ps = bank("x1", (o_normed, G + 1))
                                for t in range(TB):
                                    mm = pe.transpose(ps[:, t * P:(t + 1) * P], osb[:, t * P:(t + 1) * P], ident[:])
                                mm.then_inc(o_turned, 1)
                        if s in (7, 8) and exists(b - 1):
                            c = s - 7
                            pe.wait_ge(o_normed, b * GROUPS)
                            ps = bank("x1", (on_split, (b - 1) * KC + c + 1))
                            for t in range(TB):
                                mm = pe.transpose(ps[:, t * P:(t + 1) * P], on[:, t, c * P:(c + 1) * P], ident[:])
                            mm.then_inc(on_turned, 1)
                        if s in (11, 12) and exists(b - 1):
                            i = s - 11
                            pe.wait_ge(on_split, b * KC)
                            ps = bank("x1", (y_evac, (b - 1) * 2 + i + 1))
                            for t in range(2):
                                for c in range(KC):
                                    tok = slice((2 * i + t) * P, (2 * i + t + 1) * P)
                                    mm = product(pe, ps[:, t * D:(t + 1) * D], [o[:, c, tok] for o in ot],
                                                 [w[:, c, :] for w in wo], c == 0, c == KC - 1)
                            mm.then_inc(y_made, 1)

                over_batches(pe, body, -2, (2, 14), NB)

            @block.scalar
            def _(act):
                def body(b, par=None):
                    for s in range(H):
                        g, j = divmod(s, GH)
                        if j == 0:
                            bt, gt = (b, g - 2) if g >= 2 else (b - 1, g + 2)
                            if exists(bt):
                                G = bt * GROUPS + gt
                                act.wait_ge(pv_done, G + 1)
                                at(act, o_turned, G)
                                act.activation(osb[:], o_ps[:, 0, :], ACT.Copy).then_inc(o_evac, 1)
                        if exists(b):
                            if j == 0:
                                at(act, pv_done, b * GROUPS + g - 1)
                            for c in range(NE):
                                act.wait_ge(e_scored, (b * H + s) * NE + c + 1)
                                act.activation(probs[:, g % 2, j, c * S:c * S + width[c]], e_ps[:, e_bank(s, c), 0:width[c]],
                                               ACT.Exp, scale=SCALE).then_inc(e_exped, 1)
                        if s == 0 and exists(b + 1):
                            src = rot if causal else qf
                            if causal:
                                act.wait_ge(summed, (b + 1) * 2 + 1)
                            else:
                                act.wait_ge(qk_evac, (b + 1) * NQ + 2)
                            at(act, q_written, (b + 1) * DMA)
                            act.activation(q_parts[:, 0], src[:], ACT.Copy).then_inc(q_hi, 1)
                        if s == 3 and exists(b + 1):
                            if causal:
                                act.wait_ge(summed, (b + 1) * 2 + 2)
                                at(act, k_written, (b + 1) * DMA)
                                act.activation(k_parts[:, 0], rot[:], ACT.Copy).then_inc(k_hi, 1)
                            else:
                                act.wait_ge(qk_evac, (b + 2) * NQ)
                                at(act, ks_landed, (b + 1) * 3 * DMA)
                                act.activation(k_parts[:, 0], kf[:], ACT.Copy).then_inc(k_hi, 1)
                        if s in (8, 9) and exists(b + 2):
                            c = s - 8
                            act.wait_ge(xt_turned, (b + 2) * KC + c + 1)
                            at(act, v_made, (b + 2) * NV)
                            act.activation(xt[0][:, c, :], x0_ps[:, 0, :], ACT.Copy).then_inc(xt_hi, 1)
                        if s in (7, 8) and exists(b - 1):
                            c = s - 7
                            act.wait_ge(on_turned, (b - 1) * KC + c + 1)
                            at(act, y_made, (b - 1) * 2)
                            act.activation(ot[0][:, c, :], x1_ps[:, 0, :], ACT.Copy).then_inc(on_hi, 1)
                        if 10 <= s < 10 + NQ and exists(b + 2):
                            i = s - 10
                            act.wait_ge(qk_made, (b + 2) * NQ + i + 1)
                            if causal:
                                at(act, roped, ((b + 1) * 2 + i // 2 + 1) * 4)
                                dst, n = (qf, kf)[i // 2][:, i % 2, :], P
                            elif i < 2:
                                at(act, q_split, b + 2)
                                dst, n = qf[:, i, :], P
                            else:
                                at(act, k_split, b + 2)
                                dst, n = kf[:], HD
                            act.activation(dst, x0_ps[0:n, 0, :], ACT.Identity, bias=bqk[0:n, i:i + 1]).then_inc(qk_evac, 1)

                over_batches(act, body, -2, (2, 14), NB)

            @block.vector
            def _(dve):
                chain = Chain(dve, dve_order, 2 * (GROUPS * 3 + 2 * 3))

                def body(b, par=None):
                    par = b % 2 if isinstance(b, int) else par

                    def normalise(i):
                        dve.wait_ge(rstd_made, (b - 1) * 2 + i + 1)
                        at(dve, stored, (b - 1) * DMA)
                        for t in range(2):
                            n = 2 * i + t
                            ins = dve.tensor_scalar(yo[:, n, :], hb[:, i, t, :], mv[:, n, 0:1], rstd[:, n:n + 1],
                                                    ALU.subtract, ALU.mult)
                        ins.then_inc(y_normed, 1)

                    def other_work(s):
                        g, j = divmod(s, GH)
                        if s in (4, 6) and exists(b + 1) and (s - 4) // 2 < NV:
                            i = (s - 4) // 2
                            n = TB // NV
                            dve.wait_ge(v_made, (b + 1) * NV + i + 1)
                            src = x0_ps[:, 0, 0:n * VC].rearrange("p (t h d) -> p t h d", t=n, d=HD)
                            dst = vo[:, 1 - par, i * n:(i + 1) * n, :, 0:HD]
                            bias = spread(bv[:], [[0, n], [HD, KVH], [1, HD]])
                            dve.tensor_tensor(dst, src, bias, ALU.add).then_inc(v_evac, 1)
                        if s in (8, 9) and exists(b + 2):
                            c = s - 8
                            dve.wait_ge(xt_hi, (b + 2) * KC + c + 1)
                            dve.tensor_tensor(xt[1][:, c, :], x0_ps[:, 0, :], xt[0][:, c, :],
                                              ALU.subtract).then_inc(xt_split, 1)
                        if s % GH == 1:
                            bt, gt = (b, g + 1) if g + 1 < GROUPS else (b + 1, 0)
                            if exists(bt):
                                G = bt * GROUPS + gt
                                dve.wait_ge(mx_turned, G + 1)
                                at(dve, max_landed, G * 2 * DMA)
                                mt = x1_ps[0:GH * TB, 0, 0:P]
                                chain.then(dve.tensor_copy(mh[:, 0, :], mt))
                                dve.tensor_tensor(mh[:, 1, :], mt, mh[:, 0, :], ALU.subtract).then_inc(mx_split, 1)
                        if s % GH == 2:
                            bt, gt = (b, g - 2) if g >= 2 else (b - 1, g + 2)
                            if exists(bt):
                                dve.wait_ge(o_turned, bt * GROUPS + gt + 1)
                                o4 = x1_ps[:, 0, :].rearrange("p (t h e) -> p t h e", t=TB, h=GH)
                                sums = o4[:, :, :, HD:HD + 1].rearrange("p t h e -> p t (h e)")
                                d4 = den[:, 0, :].rearrange("p (t h) -> p t h", t=TB)
                                chain.then(dve.tensor_scalar(d4, sums, SUM_EPS if causal else 0.0, None, ALU.add))
                                chain.then(dve.reciprocal(den[:, 1, :], den[:, 0, :]))
                                r = spread(den[:, 1, :], [[GH, TB], [1, GH], [0, HD]])
                                o = on[:, :, gt * GH * HD:(gt + 1) * GH * HD].rearrange("p t (h d) -> p t h d", d=HD)
                                dve.tensor_tensor(o, o4[:, :, :, 0:HD], r, ALU.mult).then_inc(o_normed, 1)
                        if s == 0 and exists(b + 1):
                            dve.wait_ge(q_hi, b + 2)
                            dve.tensor_tensor(q_parts[:, 1], (rot if causal else qf)[:], q_parts[:, 0],
                                              ALU.subtract).then_inc(q_split, 1)
                        if s == 3 and exists(b + 1):
                            dve.wait_ge(k_hi, b + 2)
                            kp = k_parts
                            dve.tensor_tensor(kp[:, 1], (rot if causal else kf)[:], kp[:, 0],
                                              ALU.subtract).then_inc(k_split, 1)
                        if s in (7, 8) and exists(b - 1):
                            c = s - 7
                            dve.wait_ge(on_hi, (b - 1) * KC + c + 1)
                            dve.tensor_tensor(ot[1][:, c, :], x1_ps[:, 0, :], ot[0][:, c, :],
                                              ALU.subtract).then_inc(on_split, 1)
                        if s in (11, 12) and exists(b - 1):
                            i = s - 11
                            dve.wait_ge(y_made, (b - 1) * 2 + i + 1)
                            dve.wait_ge(xr_biased, b)
                            src = x1_ps[:, 0, :].rearrange("p (t d) -> p t d", t=2)
                            dve.tensor_tensor(hb[:, i], src, xr[:, 2 * i:2 * i + 2, :], ALU.add).then_inc(y_evac, 1)
                            dve.wait_ge(y_evac, (b - 1) * 2 + i + 1)
                            dve.bn_stats(stats[:, 2 * i, :], hb[:, i, 0, :])
                            chain.then(dve.bn_stats(stats[:, 2 * i + 1, :], hb[:, i, 1, :]), dve_passed)
                            dve.bn_aggr(mv[:, 2 * i, :], stats[:, 2 * i, :])
                            chain.then(dve.bn_aggr(mv[:, 2 * i + 1, :], stats[:, 2 * i + 1, :]))
                            dve.tensor_scalar(veps[:, 2 * i:2 * i + 2],
                                              mv[:, 2 * i:2 * i + 2, 1:2].rearrange("p t e -> p (t e)"),
                                              LN_EPS, None, ALU.add).then_inc(var_made, 1)
                        if s in (12, 13) and exists(b - 1):
                            normalise(s - 12)

                    for s in range(H):
                        bm, hm = (b, s + LEAD) if s + LEAD < H else (b + 1, s + LEAD - H)
                        for qb in range(TB):
                            if qb == 2 and s:
                                other_work(s - 1)
                            if exists(bm):
                                n = (bm * H + hm) * TB + qb
                                if causal:
                                    at(dve, m_reduced, n - 1)
                                    at_alone(dve, m_scored, n + 1, dve_passed)
                                else:
                                    dve.wait_ge(m_scored, n + 1)
                                w = (qb + 1) * P
                                col = mx[:, hm * TB + qb:hm * TB + qb + 1]
                                if causal:
                                    dve.tensor_tensor_reduce(junk[:, qb % 2, 0:w], m_ps[:, qb % 2, 0:w],
                                                             mask[:, 512 - w:512], 1.0, MASKED,
                                                             ALU.add, ALU.max, col).then_inc(m_reduced, 1)
                                else:
                                    dve.tensor_reduce(col, m_ps[:, qb % 2, :], AX.X, ALU.max).then_inc(m_reduced, 1)

                chain.per_two = 2 * (GROUPS * 3 + 2 * 2)
                over_batches(dve, body, -2, (2, 14), NB, chain)

            @block.gpsimd
            def _(pool):
                def body(b, par=None):
                    for s in range(H):
                        g, j = divmod(s, GH)
                        if causal and exists(b):
                            at_alone(pool, e_exped, (b * H + s + 1) * NE, pool_passed)
                            for kbs, step in (((0, 1, 2), 512), ((3,), 0)):
                                starts = sorted(start_of[kb] for kb in range(TB))
                                first = 896 if len(kbs) == 1 else 0
                                dims = [[512, 3], [1, P]] if first == 0 else [[1, P]]
                                blk = spread(probs[:, g % 2, j, first:first + 1], dims)
                                pattern = [[0, 3], [1, P]] if first == 0 else [[1, P]]
                                ins = pool.affine_select(out=blk, in_=blk, pattern=pattern, compare_op=ALU.is_ge,
                                                         fill=0.0, base=0, channel_multiplier=-1)
                            ins.then_inc(masked, 1)
                        if causal:
                            for slot, which, ahead, part in ((12, 0, 2, 0), (13, 0, 2, 1), (15, 1, 2, 0), (0, 1, 1, 1)):
                                bt = b + ahead
                                if s == slot and exists(bt):
                                    src = (qf, kf)[which]
                                    if part == 0:
                                        pool.wait_ge(qk_evac, bt * NQ + 2 * which + 2)
                                        at(pool, summed, bt * 2 + which)
                                    for e in range(2):
                                        pool.tensor_tensor(prods[:, 2 * part + e, :], src[:, e, :],
                                                           cs[:, (e + part) % 2, :], ALU.mult).then_inc(roped, 1)
                            for slot, which, ahead in ((14, 0, 2), (1, 1, 1)):
                                bt = b + ahead
                                if s == slot and exists(bt):
                                    pool.wait_ge(roped, (bt * 2 + which + 1) * 4)
                                    at(pool, *((q_split, bt + 1) if which else (k_split, bt)))
                                    pool.tensor_tensor(rot[:, 0, :], prods[:, 0, :], prods[:, 1, :], ALU.subtract)
                                    pool.tensor_tensor(rot[:, 1, :], prods[:, 2, :], prods[:, 3, :],
                                                       ALU.add).then_inc(summed, 1)
                        if s == 8 and exists(b - 1):
                            pool.wait_ge(xr_landed, b * DMA)
                            pool.tensor_tensor(xr[:], xr[:], spread(bo[:], [[0, TB], [1, D]]), ALU.add).then_inc(xr_biased, 1)
                        if s in (11, 12) and exists(b - 1):
                            i = s - 11
                            pool.wait_ge(var_made, (b - 1) * 2 + i + 1)
                            pool.tensor_tensor(rstd[:, 2 * i:2 * i + 2], veps[:, 2 * i:2 * i + 2], mhalf[:],
                                               ALU.pow).then_inc(rstd_made, 1)

                over_batches(pool, body, -2, (2, 14), NB)

            @block.sync
            def _(sp):
                def rows(x, b):
                    return x[bass.ds(b, 1)].rearrange("o (t p) d -> p (o t) d", p=P)

                def body(b, par=None):
                    par = b % 2 if isinstance(b, int) else par

                    for s in range(H):
                        g = s // GH
                        if s % GH == 1:
                            bt, gt = (b, g + 1) if g + 1 < GROUPS else (b + 1, 0)
                            if exists(bt):
                                sp.wait_ge(mx_split, bt * GROUPS + gt + 1)
                                for r in range(2):
                                    sp.dma_start(qs[MAX_ROW + r:MAX_ROW + r + 1, gt * GH:(gt + 1) * GH, :].bitcast(F32),
                                                 mh[:, r, :].bitcast(F32)).then_inc(max_landed, DMA)
                        if s == 1 and exists(b + 1):
                            sp.wait_ge(q_split, b + 2)
                            sp.dma_start(q_dram[bass.ds(b + 1, 1)].rearrange("o r (e i) h t -> (o i h) (r e) t", e=2),
                                         q_parts.rearrange("p r e t -> p (r e) t").bitcast(F32)).then_inc(q_written, DMA)
                        if s == 4 and exists(b + 1):
                            sp.wait_ge(k_split, b + 2)
                            if causal:
                                sp.dma_start(k_dram[bass.ds(b + 1, 1)].rearrange("o r (e i) h t -> (o i h) (r e) t", e=2),
                                             k_parts.rearrange("p r e t -> p (r e) t").bitcast(F32)).then_inc(k_written, DMA)
                                sp.wait_ge(k_written, (b + 2) * DMA)
                            else:
                                at(sp, e_scored, b * H * NE)
                                for n, r in enumerate((0, 1, 0)):
                                    sp.dma_start(ks[n * HD:(n + 1) * HD, 1 - par, :].bitcast(F32),
                                                 k_parts[:, r, :].bitcast(F32)).then_inc(ks_landed, DMA)
                            sp.wait_ge(q_written, (b + 2) * DMA)
                        if s in (4, 7, 11, 15) and exists(b + 1):
                            gt = (4, 7, 11, 15).index(s)
                            at(sp, e_scored, (b * H + gt * GH + GH) * NE)
                            hs = slice(gt * GH, (gt + 1) * GH)
                            for n, (rq, rk) in enumerate(((0, 0), (0, 1), (1, 0))):
                                for dram, stack, r in ((q_dram, qs, rq), (k_dram, ks, rk))[:2 if causal else 1]:
                                    sp.dma_start(stack[n * HD:(n + 1) * HD, hs, :].bitcast(F32),
                                                 dram[bass.ds(b + 1, 1), r, :, hs, :].rearrange("o d h t -> (o d) h t")
                                                 ).then_inc(stack_landed[gt], DMA)
                        if s == 4 and exists(b + 2):
                            at(sp, xt_turned, (b + 2) * KC)
                            sp.dma_start(xn[:], rows(x_in, b + 2)).then_inc(xn_landed, DMA)
                        if s == 5 and exists(b - 1):
                            at(sp, y_evac, (b - 1) * 2)
                            sp.dma_start(xr[:], rows(x_in, b - 1)).then_inc(xr_landed, DMA)
                        if s == 14 and exists(b - 1):
                            sp.wait_ge(y_normed, b * 2)
                            sp.dma_start(rows(x_out, b - 1), yo[:]).then_inc(stored, DMA)

                over_batches(sp, body, -2, (2, 14), NB)
                sp.wait_ge(stored, NB * DMA)


def expert_layer(nc, sems, passed, name, x_in, x_out, gate, up_w, down_w, E, TOP, plain, glu, ident_in):
    U = plain + glu
    scaled = TOP == 1
    kinds = ["plain"] * plain + ["glu"] * glu
    DC = [2] * plain + [1] * glu
    d_first = [sum(DC[:u]) for u in range(U)]
    PAD = 8
    with ExitStack() as ctx:
        def sb(n, shape, dt=F32):
            return ctx.enter_context(nc.sbuf_tensor(f"{name}_{n}", shape, dt))

        def sem(n):
            return sems.enter_context(nc.semaphore(f"{name}_{n}"))

        w1 = [sb(f"w_up_{p}", [P, U, KC, 2 * P], F32R) for p in ("hi", "lo")]
        w2 = [sb(f"w_down_{p}", [P, sum(DC), D], F32R) for p in ("hi", "lo")]
        wg = [sb(f"w_gate_{p}", [P, KC, E], F32R) for p in ("hi", "lo")]
        xn2 = sb("x", [P, 2, TB, D])
        xt2 = [sb(f"xT_{p}", [P, 2, KC, S], F32R) for p in ("hi", "lo")]
        hf = sb("h", [P, 2 * S])
        ht = [sb(f"hT_{p}", [P, 2, 2 * S], F32R) for p in ("hi", "lo")]
        acc = sb("acc", [P, TB, D])
        yo = sb("y_out", [P, TB, D])
        ident = sb("identity", [P, P])
        lg = sb("logits", [P, TB, E + PAD])
        left = sb("logits_left", [P, TB, E + PAD])
        top8 = sb("top8", [P, TB, 8])
        top = sb("to_replace", [P, TB, 8])
        low = sb("shifted", [P, TB, E])
        ex = sb("exps", [P, TB, E])
        wt2 = sb("weights", [P, 2, TB, E])
        tot = sb("totals", [P, 2, TB])
        stats = sb("stats", [P, TB, 6])
        mv = sb("mean_var", [P, TB, 2])
        veps = sb("var_eps", [P, TB])
        rstd = sb("rstd", [P, TB])
        mhalf = sb("minus_half", [P, TB])
        xs = sb("x_scaled", [P, TB, D]) if scaled else None

        def psum(n, banks):
            return ctx.enter_context(nc.psum_tensor(f"{name}_{n}", [P, banks, S], F32))

        h_ps = [psum("ps_h0", 2), psum("ps_h1", 2)]
        y_ps = psum("ps_y", 2)
        t_ps = psum("ps_turn", 2)

        const_landed, const_made = sem("const_landed"), sem("const_made")
        x_landed, stored = sem("x_landed"), sem("stored")
        x_turned, xt_hi, xt_split = sem("x_turned"), sem("xt_hi"), sem("xt_split")
        routed, logits_read, shifted, exped, weighed, x_scaled = (
            sem("routed"), sem("logits_read"), sem("shifted"), sem("exped"), sem("weighed"), sem("x_scaled"))
        h_made, h_silu, h_whole, h_hi, h_split = (
            sem("h_made"), sem("h_silu"), sem("h_whole"), sem("h_hi"), sem("h_split"))
        y_made, y_added, var_made, rstd_made, y_normed = (
            sem("y_made"), sem("y_added"), sem("var_made"), sem("rstd_made"), sem("y_normed"))
        dve_order = sem("dve_order")
        dve_passed, pool_passed = passed

        turns = 2 * KC if scaled else KC
        TURN_AT, ROUTE_AT, WEIGH_AT, SCALED_AT = 2, 4, 5, 6

        stage = sb("stage", [P, 2 * 512])
        specs = [(gate, *[w.rearrange("p c n -> p (c n)") for w in wg])]
        for u in range(U):
            specs.append((up_w[u], *[w[:, u].rearrange("p c n -> p (c n)") for w in w1]))
            specs.append((down_w[:, d_first[u]:d_first[u] + DC[u], :].rearrange("p c n -> p (c n)"),
                          *[w[:, d_first[u]:d_first[u] + DC[u], :].rearrange("p c n -> p (c n)") for w in w2]))
        load_split_weights(nc, sems, specs, stage, name)

        with nc.Block() as block:
            @block.sync
            def _(sp):
                sp.dma_start(ident[:], ident_in).then_inc(const_landed, DMA)
                sp.wait_ge(const_landed, DMA)

            @block.gpsimd
            def _(pool):
                pool.memset(mhalf[:], -0.5)
                pool.memset(lg[:], MASKED)

            @block.vector
            def _(dve):
                dve.memset(top[:], MASKED)

        def unit(b, u):
            return b * U + u

        with nc.Block() as block:
            @block.tensor
            def _(pe):
                def turn(b, n, src):
                    at(pe, xt_split, b * turns + n - 1)
                    for t in range(TB):
                        mm = pe.transpose(t_ps[:, n % 2, t * P:(t + 1) * P], src[:, t, (n % KC) * P:(n % KC + 1) * P],
                                          ident[:])
                    mm.then_inc(x_turned, 1)

                def turn_x(b, par):
                    pe.wait_ge(x_landed, (b + 1) * DMA)
                    at(pe, logits_read, b)
                    for c in range(KC):
                        turn(b, c, xn2[:, par])

                def route(b, par):
                    pe.wait_ge(xt_split, b * turns + KC)
                    for t in range(TB):
                        for c in range(KC):
                            mm = product(pe, t_ps[:, 0, t * E:(t + 1) * E],
                                         [x[:, par, c, t * P:(t + 1) * P] for x in xt2],
                                         [w[:, c, :] for w in wg], c == 0, c == KC - 1)
                    mm.then_inc(routed, 1)

                def turn_scaled(b):
                    pe.wait_ge(x_scaled, b + 1)
                    pe.wait_ge(logits_read, b + 1)
                    for c in range(KC):
                        turn(b, KC + c, xs)

                def up(b, u, par):
                    n = unit(b, u)
                    if u == 0:
                        pe.wait_ge(xt_split, (b + 1) * turns)
                    at(pe, h_split, n - 1)
                    for m in range(2):
                        for c in range(KC):
                            mm = product(pe, h_ps[u % 2][:, m, :], [w[:, u, c, m * P:(m + 1) * P] for w in w1],
                                         [x[:, par, c, :] for x in xt2], c == 0, c == KC - 1)
                    mm.then_inc(h_made, 1)

                def down(b, u):
                    n = unit(b, u)
                    pe.wait_ge(h_split, n + 1)
                    for i in range(2):
                        at(pe, y_added, 2 * n + i - 1)
                        for t in range(2):
                            tok = (2 * i + t) * P
                            for c in range(DC[u]):
                                mm = product(pe, y_ps[:, i, t * D:(t + 1) * D],
                                             [h[:, u % 2, c * S + tok:c * S + tok + P] for h in ht],
                                             [w[:, d_first[u] + c, :] for w in w2], c == 0, c == DC[u] - 1)
                        mm.then_inc(y_made, 1)

                def body(b, par=None):
                    par = b % 2 if isinstance(b, int) else par
                    if exists(b):
                        for u in range(U):
                            up(b, u, par)
                            if u == TURN_AT and exists(b + 1):
                                turn_x(b + 1, 1 - par)
                            if u == ROUTE_AT and exists(b + 1):
                                route(b + 1, 1 - par)
                            if u == SCALED_AT and scaled and exists(b + 1):
                                turn_scaled(b + 1)
                            if u or exists(b - 1):
                                down(*((b, u - 1) if u else (b - 1, U - 1)))
                    elif b < 0:
                        turn_x(0, 0)
                        route(0, 0)
                        if scaled:
                            turn_scaled(0)
                    else:
                        down(b - 1, U - 1)

                over_batches(pe, body, -1, (2, 14), NB)

            @block.scalar
            def _(act):
                def hi_parts(b, par, chunks):
                    for n in chunks:
                        act.wait_ge(x_turned, b * turns + n + 1)
                        if n == 0:
                            at(act, h_made, unit(b - 1, 0))
                        if n == KC:
                            act.wait_ge(routed, b + 1)
                        act.activation(xt2[0][:, par, n % KC, :], t_ps[:, n % 2, :], ACT.Copy).then_inc(xt_hi, 1)

                def exponentials(b):
                    act.wait_ge(shifted, b + 1)
                    n = E if TOP > 1 else 1
                    act.activation(ex[:, :, 0:n], low[:, :, 0:n], ACT.Exp).then_inc(exped, 1)

                def hidden(b, u):
                    n = unit(b, u)
                    act.wait_ge(h_made, n + 1)
                    w = 2 * S if kinds[u] == "plain" else S
                    at(act, h_split, n)
                    act.activation(hf[:, 0:w], h_ps[u % 2].rearrange("p m s -> p (m s)")[:, 0:w],
                                   ACT.Silu).then_inc(h_silu, 1)
                    if kinds[u] == "glu":
                        act.wait_ge(h_whole, b * glu + (u - plain) + 1)
                    else:
                        act.wait_ge(h_silu, n + 1)
                    at(act, y_made, 2 * (n - 1))
                    act.activation(ht[0][:, u % 2, 0:w], hf[:, 0:w], ACT.Copy).then_inc(h_hi, 1)

                def body(b, par=None):
                    par = b % 2 if isinstance(b, int) else par
                    if exists(b):
                        for u in range(U):
                            hidden(b, u)
                            if u == TURN_AT and exists(b + 1):
                                hi_parts(b + 1, 1 - par, range(KC))
                            if u == WEIGH_AT and exists(b + 1):
                                exponentials(b + 1)
                            if u == SCALED_AT and scaled and exists(b + 1):
                                hi_parts(b + 1, 1 - par, range(KC, turns))
                    elif b < 0:
                        hi_parts(0, 0, range(KC))
                        exponentials(0)
                        hi_parts(0, 0, range(KC, turns))

                over_batches(act, body, -1, (2, 14), NB)

            @block.vector
            def _(dve):
                chain = Chain(dve, dve_order, 0)

                def lo_parts(b, par, chunks):
                    for n in chunks:
                        dve.wait_ge(xt_hi, b * turns + n + 1)
                        dve.tensor_tensor(xt2[1][:, par, n % KC, :], t_ps[:, n % 2, :], xt2[0][:, par, n % KC, :],
                                          ALU.subtract).then_inc(xt_split, 1)

                def choose(b):
                    dve.wait_ge(routed, b + 1)
                    dve.tensor_copy(lg[:, :, 0:E], t_ps[:, 0, 0:TB * E].rearrange("p (t e) -> p t e", t=TB)
                                    ).then_inc(logits_read, 1)
                    at_alone(dve, logits_read, b + 1, dve_passed)
                    for t in range(TB):
                        ins = dve.max(top8[:, t, :], lg[:, t, 0:E])
                    chain.then(ins)
                    chain.then(dve.tensor_copy(top[:, :, 0:TOP], top8[:, :, 0:TOP]), dve_passed)
                    for t in range(TB):
                        ins = dve.match_replace(left[:, t, :], top[:, t, :], lg[:, t, :], -3.3e38)
                    chain.then(ins)
                    if TOP > 1:
                        biggest = spread(top8[:], [[8, TB], [0, E]])
                        dve.tensor_tensor(low[:], lg[:, :, 0:E], biggest, ALU.subtract).then_inc(shifted, 1)
                    else:
                        dve.tensor_scalar(low[:, :, 0:1], top8[:, :, 0:1], -1.0, None, ALU.mult).then_inc(shifted, 1)

                def weigh(b, par):
                    wt = wt2[:, par]
                    chosen = dve.tensor_tensor(wt, left[:, :, 0:E], lg[:, :, 0:E], ALU.not_equal)
                    if TOP > 1:
                        chain.then(chosen)
                        dve.wait_ge(exped, b + 1)
                        chain.then(dve.tensor_tensor(wt, wt, ex[:], ALU.mult))
                        chain.then(dve.tensor_reduce(tot[:, 0, :], wt, AX.X, ALU.add))
                        chain.then(dve.reciprocal(tot[:, 1, :], tot[:, 0, :]))
                        dve.tensor_tensor(wt, wt, spread(tot[:, 1, :], [[1, TB], [0, E]]),
                                          ALU.mult).then_inc(weighed, 1)
                    else:
                        chosen.then_inc(weighed, 1)
                        dve.wait_ge(exped, b + 1)
                        chain.then(dve.tensor_scalar(tot[:, 0, :], ex[:, :, 0:1].rearrange("p t e -> p (t e)"),
                                                     1.0, None, ALU.add))
                        chain.then(dve.reciprocal(tot[:, 1, :], tot[:, 0, :]))
                        for t in range(TB):
                            ins = dve.tensor_scalar(xs[:, t, :], xn2[:, par, t, :], tot[:, 1, t:t + 1], None, ALU.mult)
                        ins.then_inc(x_scaled, 1)

                def hidden(b, u):
                    n = unit(b, u)
                    w = 2 * S if kinds[u] == "plain" else S
                    if kinds[u] == "glu":
                        dve.wait_ge(h_silu, n + 1)
                        dve.tensor_tensor(hf[:, 0:S], hf[:, 0:S], h_ps[u % 2][:, 1, :], ALU.mult).then_inc(h_whole, 1)
                    dve.wait_ge(h_hi, n + 1)
                    dve.tensor_tensor(ht[1][:, u % 2, 0:w], hf[:, 0:w], ht[0][:, u % 2, 0:w],
                                      ALU.subtract).then_inc(h_split, 1)

                def add_up(b, u, par):
                    n = unit(b, u)
                    if u == 0:
                        dve.wait_ge(weighed, b + 1)
                    else:
                        dve.wait_ge(y_added, 2 * n)
                    for i in range(2):
                        dve.wait_ge(y_made, 2 * n + i + 1)
                        for t in range(2):
                            k = 2 * i + t
                            weight = wt2[:, par, k, u:u + 1] if u < E else 1.0
                            ins = dve.scalar_tensor_tensor(out=acc[:, k, :], in0=y_ps[:, i, t * D:(t + 1) * D],
                                                           scalar=weight, in1=(acc if u else xn2[:, par])[:, k, :],
                                                           op0=ALU.mult, op1=ALU.add)
                        ins.then_inc(y_added, 1)

                def moments(b):
                    dve.wait_ge(y_added, (b + 1) * U * 2)
                    for t in range(TB):
                        ins = dve.bn_stats(stats[:, t, :], acc[:, t, :])
                    chain.then(ins, dve_passed)
                    for t in range(TB):
                        ins = dve.bn_aggr(mv[:, t, :], stats[:, t, :])
                    chain.then(ins)
                    dve.tensor_scalar(veps[:], mv[:, :, 1:2].rearrange("p t e -> p (t e)"), LN_EPS, None,
                                      ALU.add).then_inc(var_made, 1)

                def normalise(b):
                    dve.wait_ge(rstd_made, b + 1)
                    at(dve, stored, b * DMA)
                    for t in range(TB):
                        ins = dve.tensor_scalar(yo[:, t, :], acc[:, t, :], mv[:, t, 0:1], rstd[:, t:t + 1],
                                                ALU.subtract, ALU.mult)
                    ins.then_inc(y_normed, 1)
                    dve.wait_ge(y_normed, b + 1)

                def body(b, par=None):
                    par = b % 2 if isinstance(b, int) else par
                    if exists(b):
                        for u in range(U):
                            hidden(b, u)
                            if u == TURN_AT and exists(b + 1):
                                lo_parts(b + 1, 1 - par, range(KC))
                            if u == ROUTE_AT and exists(b + 1):
                                choose(b + 1)
                            if u == WEIGH_AT and exists(b + 1):
                                weigh(b + 1, 1 - par)
                            if u == SCALED_AT and scaled and exists(b + 1):
                                lo_parts(b + 1, 1 - par, range(KC, turns))
                            if u == 1 and exists(b - 1):
                                normalise(b - 1)
                            if u:
                                add_up(b, u - 1, par)
                            elif exists(b - 1):
                                add_up(b - 1, U - 1, 1 - par)
                                moments(b - 1)
                    elif b < 0:
                        lo_parts(0, 0, range(KC))
                        choose(0)
                        weigh(0, 0)
                        lo_parts(0, 0, range(KC, turns))
                    else:
                        add_up(b - 1, U - 1, 1 - par)
                        moments(b - 1)
                        normalise(b - 1)

                chain.per_two = 2 * ((7 if TOP > 1 else 5) + 2)
                over_batches(dve, body, -1, (2, 14), NB, chain)

            @block.gpsimd
            def _(pool):
                def body(b, par=None):
                    if exists(b - 1):
                        pool.wait_ge(var_made, b)
                        pool.tensor_tensor(rstd[:], veps[:], mhalf[:], ALU.pow).then_inc(rstd_made, 1)

                over_batches(pool, body, -1, (2, 14), NB)

            @block.sync
            def _(sp):
                def rows(x, b):
                    return x[bass.ds(b, 1)].rearrange("o (t p) d -> p (o t) d", p=P)

                def body(b, par=None):
                    par = b % 2 if isinstance(b, int) else par
                    if exists(b + 1):
                        at(sp, y_added, unit(b - 1, 0) * 2 + 2)
                        at(sp, x_landed, (b + 1) * DMA)
                        sp.dma_start(xn2[:, 1 - par], rows(x_in, b + 1)).then_inc(x_landed, DMA)
                    if exists(b - 1):
                        sp.wait_ge(y_normed, b)
                        sp.dma_start(rows(x_out, b - 1), yo[:]).then_inc(stored, DMA)

                over_batches(sp, body, -1, (2, 14), NB)
                sp.wait_ge(stored, NB * DMA)


def phase(nc, sems, passed, which, x, out, a):
    if which == "a0":
        attention_layer(nc, sems, passed, "l0", True, x, out, (a["l0_wqk"], a["l0_wv"]), (a["l0_bqk"], a["l0_bv"]),
                        a["l0_wo"], a["l0_bo"], (a["cos_sin"],), a["ident"])
    if which == "e0":
        expert_layer(nc, sems, passed, "e0", x, out, a["e0_gate"], a["e0_up"], a["e0_down"], 16, 4, 16, 2, a["ident"])
    if which == "a1":
        attention_layer(nc, sems, passed, "l1", False, x, out, (a["l1_wqk"], a["l1_wv"]), (a["l1_bqk"], a["l1_bv"]),
                        a["l1_wo"], a["l1_bo"], (), a["ident"])
    if which == "e1":
        expert_layer(nc, sems, passed, "e1", x, out, a["e1_gate"], a["e1_up"], a["e1_down"], 8, 1, 0, 8, a["ident"])


def program(nc, x, out, a):
    between = [nc.dram_tensor(n, [NB, S, D], F32, kind="Internal").ap() for n in ("x1", "x2", "x3")]
    stops = [x, *between, out]
    with ExitStack() as sems:
        passed = [sems.enter_context(nc.semaphore(n)) for n in ("dve_passed", "pool_passed")]
        for n, which in enumerate(("a0", "e0", "a1", "e1")):
            phase(nc, sems, passed, which, stops[n], stops[n + 1], a)


def layouts(i):
    f = {k: np.asarray(v) for k, v in i.items()}

    def chunks(w):
        return np.ascontiguousarray(w.reshape(KC, P, -1).transpose(1, 0, 2).reshape(P, -1))

    def rowwise(v, n=P):
        return np.ascontiguousarray(np.broadcast_to(v.reshape(1, -1), (n, v.size)))

    order = np.arange(D).reshape(H, HALF, 2).transpose(2, 1, 0).reshape(-1)
    one_head = np.arange(HD).reshape(HALF, 2).T.reshape(-1)
    wt = f["L0_attn_w_qkv"].T
    bq = f["L0_attn_b_qkv"]
    a = {
        "l0_wqk": chunks(np.concatenate([wt[:, :D][:, order], wt[:, D:2 * D][:, order]], 1)),
        "l0_wv": chunks(wt[:, 2 * D:]),
        "l0_bqk": np.ascontiguousarray(np.concatenate([bq[:D][order], bq[D:2 * D][order]]).reshape(4, P).T),
        "l0_bv": rowwise(bq[2 * D:]),
        "l0_wo": chunks(f["L0_attn_w_out"].T),
        "l0_bo": rowwise(f["L0_attn_b_out"]),
    }
    a["l1_wqk"] = chunks(np.concatenate([f["L1_attn_Wq"][:, order], f["L1_attn_Wk"][:, one_head]], 1))
    a["l1_wv"] = chunks(f["L1_attn_Wv"])
    pad = np.zeros(P - HD, np.float32)
    a["l1_bqk"] = np.ascontiguousarray(np.concatenate([f["L1_attn_bq"][order], f["L1_attn_bk"][one_head], pad]).reshape(3, P).T)
    a["l1_bv"] = rowwise(f["L1_attn_bv"])
    a["l1_wo"] = chunks(f["L1_attn_Wo"])
    a["l1_bo"] = rowwise(f["L1_attn_bo"])
    gu = f["L0_ffn_shared_gu"].T
    shared = [np.concatenate([gu[:, u * P:(u + 1) * P], gu[:, D + u * P:D + (u + 1) * P]], 1) for u in range(2)]
    a["e0_gate"] = chunks(f["L0_ffn_gate_w"].T)
    a["e0_up"] = np.stack([chunks(w.T) for w in f["L0_ffn_w1"]] + [chunks(w) for w in shared])
    down = np.concatenate([w.T for w in f["L0_ffn_w2"]] + [f["L0_ffn_shared_down"].T], 0)
    a["e0_down"] = np.ascontiguousarray(down.reshape(-1, P, D).transpose(1, 0, 2))
    a["e1_gate"] = chunks(f["L1_ffn_gate_w"].T)
    a["e1_up"] = np.stack([chunks(np.concatenate([g.T, u.T], 1)) for g, u in zip(f["L1_ffn_w_gate"], f["L1_ffn_w_up"])])
    a["e1_down"] = np.ascontiguousarray(f["L1_ffn_w_down"].transpose(2, 0, 1))
    inv = (10000.0 ** (-np.arange(0, HD, 2, dtype=np.float32) / HD)).astype(np.float32)
    ang = np.arange(S, dtype=np.float32)[None, :] * inv[:, None]
    a["cos_sin"] = np.repeat(np.stack([np.cos(ang), np.sin(ang)], 1), H, 0).astype(np.float32)
    a["ident"] = np.eye(P, dtype=np.float32)
    return a


def kernel(**inputs):
    import concourse.bacc as bacc
    from concourse.bass_utils import run_bass_kernel_spmd

    nc = bacc.Bacc("TRN2", target_bir_lowering=False, num_devices=1, dynamic_dma_scratch_size=64)
    arrays = {"x": np.ascontiguousarray(inputs["L0_attn_x"]), **layouts(inputs)}
    aps = {n: nc.dram_tensor(n, list(v.shape), F32, kind="ExternalInput").ap() for n, v in arrays.items()}
    out = nc.dram_tensor("out", [NB, S, D], F32, kind="ExternalOutput").ap()
    program(nc, aps.pop("x"), out, aps)
    r = run_bass_kernel_spmd(nc, [arrays], core_ids=[0])
    return r.results[0]["out"]
```

```python
from contextlib import ExitStack

import numpy as np

import concourse.bass as bass
from concourse import mybir

F32, F32R, BF16 = mybir.dt.float32, mybir.dt.float32r, mybir.dt.bfloat16
ALU, ACT, AX = mybir.AluOpType, mybir.ActivationFunctionType, mybir.AxisListType

P = 128
NB, S, D = 16, 512, 256
H, HD = 16, 16
TB = S // P
KC = D // P
HALF = HD // 2
GROUPS, GH = 4, 4
SPLITS = 3
STACK = SPLITS * HD
MAX_ROW = P - 2
LEAD = 7
SCALE = 1.0 / float(np.sqrt(HD))
LN_EPS, SUM_EPS = 1e-5, 1e-8
MASKED = -3.0e38
DMA = 16


def at(eng, sem, value):
    if not isinstance(value, int) or value > 0:
        eng.wait_ge(sem, value)


def at_most(value, most):
    return min(value, most) if isinstance(value, int) else value


def at_alone(eng, sem, value, passed):
    at(eng, sem, value)
    if not isinstance(value, int):
        eng.sem_inc(passed, 1)


class Chain:

    def __init__(self, eng, sem, per_two):
        self.eng, self.sem, self.n, self.per_two = eng, sem, 0, per_two

    def then(self, instruction, alone=None):
        self.n = self.n + 1
        instruction.then_inc(self.sem, 1)
        if alone:
            at_alone(self.eng, self.sem, self.n, alone)
        else:
            self.eng.wait_ge(self.sem, self.n)


def over_batches(eng, body, first, looped, last, chain=None):
    lo, hi = looped
    for b in range(first, lo):
        body(b)
    before = chain.n if chain else 0
    with eng.Fori(0, (hi - lo) // 2) as i:
        if chain:
            chain.n = i * chain.per_two + before
        body(i * 2 + lo, 0)
        body(i * 2 + (lo + 1), 1)
    if chain:
        chain.n = before + (hi - lo) // 2 * chain.per_two
    for b in range(hi, last + 1):
        body(b)


def exists(b):
    return not isinstance(b, int) or 0 <= b < NB


def spread(ap, dims):
    return bass.AP(ap.tensor, ap.offset, [list(ap.ap[0])] + dims)


def product(pe, out, a, b, start=True, stop=True):
    pe.matmul(out, a[0], b[0], start=start, stop=False)
    pe.matmul(out, a[1], b[0], start=False, stop=False)
    return pe.matmul(out, a[0], b[1], start=False, stop=stop)


class WeightLoads:
    SLOTS = 4

    def __init__(self, nc, ctx):
        self.nc, self.n = nc, 0
        self.landed = [ctx.enter_context(nc.semaphore(f"weights_landed_{i}")) for i in range(self.SLOTS)]
        self.hi_done = ctx.enter_context(nc.semaphore("weights_hi"))
        self.lo_done = ctx.enter_context(nc.semaphore("weights_lo"))

    def load(self, specs, stage, constants, const_landed):
        landed, hi_done, lo_done, SLOTS, first = self.landed, self.hi_done, self.lo_done, self.SLOTS, self.n
        self.n = first + len(specs)
        jobs = list(enumerate(specs, first))

        def staged(n, like):
            dims = list(like.shape[1:])
            flat = stage[n % SLOTS][:, 0:int(np.prod(dims))]
            return flat if len(dims) == 1 else flat.rearrange("p (a b) -> p a b", a=dims[0])

        with self.nc.Block() as block:
            @block.sync
            def _(sp):
                for n, (src, hi, lo) in jobs:
                    if n - first >= SLOTS:
                        sp.wait_ge(lo_done, n - SLOTS + 1)
                    sp.dma_start(staged(n, src), src).then_inc(landed[n % SLOTS], DMA)
                for dst, src in constants:
                    sp.dma_start(dst, src).then_inc(const_landed, DMA)
                sp.wait_ge(const_landed, DMA * len(constants))

            @block.scalar
            def _(act):
                for n, (src, hi, lo) in jobs:
                    act.wait_ge(landed[n % SLOTS], DMA * (n // SLOTS + 1))
                    act.activation(hi, staged(n, src), ACT.Copy).then_inc(hi_done, 1)

            @block.vector
            def _(dve):
                for n, (src, hi, lo) in jobs:
                    dve.wait_ge(hi_done, n + 1)
                    dve.tensor_tensor(lo, staged(n, src), hi, ALU.subtract).then_inc(lo_done, 1)


def attention_layer(nc, sems, weights, passed, name, causal, x_in, x_out, w_qkv, b_qkv, w_out, b_out, tables, ident_in):
    NQ = 4 if causal else 3
    NV = 2 if causal else 1
    NE = 3 if causal else 4
    PW = 1280 if causal else TB * S
    KVH = H if causal else 1
    parts = [(0, 0, 0, 0), (1, 0, 128, 1), (1, 384, 384, 3), (2, 0, 256, 2)] if causal else [
        (kb, 0, 0, kb) for kb in range(TB)]
    start_of = {kb: bank * S + col for bank, col, q0, kb in parts}
    width = {0: S, 1: S, 2: 256} if causal else {kb: S for kb in range(TB)}
    VC = D if causal else HD
    E_BANKS, M_BANKS = (2, 3) if causal else (3, 2)
    row_parts = [(0, 0), (0, P), (1, 0), (2, 0)] if causal else [(qb, 0) for qb in range(TB)]
    NM = row_parts[-1][0] + 1
    last_of_part = [qb == TB - 1 or row_parts[qb + 1][0] != row_parts[qb][0] for qb in range(TB)]
    V_AT, XT_AT = ((4, 5), (7, 8)) if causal else ((4,), (8, 9))
    QK_AT, OT_AT, Y_AT, MAX_AT = 10, (7, 8), (11, 12), 1
    TURNS = ([("max", 0), ("max", 1), ("exp", 0), ("max", 2), ("max", 3), ("exp", 1), ("exp", 2), "sums", ("exp", 3)]
             if causal else
             [("exp", 0), ("max", 0), ("exp", 1), ("exp", 2), ("max", 1), "sums", ("max", 2), ("exp", 3), ("max", 3)])

    def e_bank(head, part):
        return (head * NE + part) % E_BANKS

    def m_bank(part):
        return part % M_BANKS

    with ExitStack() as ctx:
        def sb(n, shape, dt=F32):
            return ctx.enter_context(nc.sbuf_tensor(f"{name}_{n}", shape, dt))

        def sem(n):
            return sems.enter_context(nc.semaphore(f"{name}_{n}"))

        q_dram = nc.dram_tensor(f"{name}_q_stacked", [NB, 2, HD, H, S], F32, kind="Internal").ap()
        k_dram = nc.dram_tensor(f"{name}_k_stacked", [NB, 2, HD, H, S], F32, kind="Internal").ap() if causal else None

        qs = sb("q_stack", [P, H, S], F32R)
        ks = sb("k_stack", [P, H if causal else 2, S], F32R)
        probs = sb("probs", [P, 2, GH, PW])
        vo = sb("v_ones", [P, 2, TB, KVH, 32])
        xn = sb("x_to_turn", [P, TB, D])
        xr = sb("x_residual", [P, TB, D])
        xt = [sb(f"xT_{p}", [P, KC, S], F32R) for p in ("hi", "lo")]
        qf = sb("q_projected", [P, 2, S])
        kf = sb("k_projected", [P, 2, S]) if causal else sb("k_projected", [HD, S])
        q_parts = sb("q_parts", [P, 2, 2, S], F32R)
        k_parts = sb("k_parts", [P, 2, 2, S], F32R) if causal else sb("k_parts", [HD, 2, S], F32R)
        mx = sb("row_max", [P, H * TB])
        mh = sb("max_parts", [GH * TB, 2, P], F32R)
        osb = sb("o_raw", [P, S])
        on = sb("o_normed", [P, TB, D])
        ot = [sb(f"oT_{p}", [P, KC, S], F32R) for p in ("hi", "lo")]
        den = sb("denominators", [P, 2, GH * TB])
        hb = sb("h", [P, 2, 2, D])
        stats = sb("stats", [P, 4, 6])
        mv = sb("mean_var", [P, 4, 2])
        veps = sb("var_eps", [P, 4])
        rstd = sb("rstd", [P, 4])
        mhalf = sb("minus_half", [P, 2])
        yo = sb("y_out", [P, TB, D])
        bo = sb("b_out", [P, D])
        ident = sb("identity", [P, P])
        QKC = 2 * D if causal else D + HD
        wqk = [sb(f"w_qk_{p}", [P, KC, QKC], F32R) for p in ("hi", "lo")]
        wv = [sb(f"w_v_{p}", [P, KC, VC], F32R) for p in ("hi", "lo")]
        wo = [sb(f"w_o_{p}", [P, KC, D], F32R) for p in ("hi", "lo")]
        bqk = sb("b_qk", [P, NQ])
        bv = sb("b_v", [P, VC])
        if causal:
            prods = sb("rope_products", [P, 4, S])
            rot = sb("rope_sums", [P, 2, S])
            cs = sb("cos_sin", [P, 2, S])
            mask = sb("causal_mask", [P, S], BF16)
            junk = sb("junk", [P, NM * S], BF16)

        def psum(n, banks):
            return ctx.enter_context(nc.psum_tensor(f"{name}_{n}", [P, banks, S], F32))

        m_ps = psum("ps_max", M_BANKS)
        e_ps = psum("ps_exp", E_BANKS)
        o_ps = psum("ps_o", 1)
        x0_ps = psum("ps_x0", 1)
        x1_ps = psum("ps_x1", 1)

        const_landed, const_made, ks_filled = sem("const_landed"), sem("const_made"), sem("ks_filled")
        CONSTS = 3 if causal else 2
        xn_landed, xr_landed, xr_biased = sem("xn_landed"), sem("xr_landed"), sem("xr_biased")
        q_written, k_written, max_landed = sem("q_written"), sem("k_written"), sem("max_landed")
        stack_landed = [sem(f"stack_landed_{g}") for g in range(GROUPS)]
        ks_landed, stored = sem("ks_landed"), sem("stored")
        m_scored, m_reduced, e_scored, e_exped, masked = (
            sem("m_scored"), sem("m_reduced"), sem("e_scored"), sem("e_exped"), sem("masked"))
        pv_done, o_evac, o_turned, o_normed = sem("pv_done"), sem("o_evac"), sem("o_turned"), sem("o_normed")
        mx_turned, mx_split = sem("mx_turned"), sem("mx_split")
        xt_turned, xt_hi, xt_split = sem("xt_turned"), sem("xt_hi"), sem("xt_split")
        qk_made, qk_evac, v_made, v_evac = sem("qk_made"), sem("qk_evac"), sem("v_made"), sem("v_evac")
        roped, summed = sem("roped"), sem("summed")
        q_hi, q_split, k_hi, k_split = sem("q_hi"), sem("q_split"), sem("k_hi"), sem("k_split")
        on_turned, on_hi, on_split = sem("on_turned"), sem("on_hi"), sem("on_split")
        y_made, y_evac, var_made, rstd_made, y_normed = (
            sem("y_made"), sem("y_evac"), sem("var_made"), sem("rstd_made"), sem("y_normed"))
        dve_order = sem("dve_order")
        dve_passed, pool_passed = passed

        stage = [probs.rearrange("p a b c -> p (a b c)")[:, i * 1024:(i + 1) * 1024] for i in range(WeightLoads.SLOTS)]
        weights.load([
            (w_qkv[0], *[w.rearrange("p c n -> p (c n)") for w in wqk]),
            (w_qkv[1], *[w.rearrange("p c n -> p (c n)") for w in wv]),
            (w_out, *[w.rearrange("p c n -> p (c n)") for w in wo]),
        ], stage, [(ident[:], ident_in), (bqk[:], b_qkv[0]), (bv[:], b_qkv[1]), (bo[:], b_out),
                   *([(cs[:], tables[0])] if causal else [])], const_landed)

        def x_start(b):
            x0 = (qk_evac, at_most((b + 2) * NQ, NB * NQ))
            if isinstance(b, int) and b <= 0:
                return x0, (mx_split, b + 1)
            return x0, (o_normed, (b - 1) * GROUPS + 2)

        with nc.Block() as block:
            @block.tensor
            def _(pe):
                def body(b, par=None):
                    par = b % 2 if isinstance(b, int) else par
                    free = dict(zip(("x0", "x1"), x_start(b)))

                    def bank(which, emptied):
                        at(pe, *free[which])
                        free[which] = emptied
                        return (x1_ps if which == "x1" else x0_ps)[:, 0, :]

                    for s in range(H):
                        g, j = divmod(s, GH)
                        bm, hm = (b, s + LEAD) if s + LEAD < H else (b + 1, s + LEAD - H)

                        def row_scores(*blocks):
                            if not exists(bm):
                                return
                            if hm % GH == 0 and blocks[0] == 0:
                                pe.wait_ge(stack_landed[hm // GH], (bm + 1) * (6 if causal else 3) * DMA)
                                if not causal and hm == 0:
                                    pe.wait_ge(ks_landed, (bm + 1) * 3 * DMA)
                            for qb in blocks:
                                part, col = row_parts[qb]
                                n = (bm * H + hm) * NM + part
                                if col == 0:
                                    at(pe, m_reduced, n - M_BANKS + 1)
                                w = (qb + 1) * P if causal else S
                                kr = ks[0:MAX_ROW, hm, 0:w] if causal else ks[0:MAX_ROW, par if bm is b else 1 - par, :]
                                mm = pe.matmul(m_ps[:, m_bank(part), col:col + w], qs[0:MAX_ROW, hm, qb * P:(qb + 1) * P],
                                               kr, start=True, stop=True)
                                if last_of_part[qb]:
                                    mm.then_inc(m_scored, 1)

                        def exp_scores(i):
                            if not exists(b):
                                return
                            if i == 0 and j == 0:
                                pe.wait_ge(max_landed, (b * GROUPS + g + 1) * 2 * DMA)
                            bk, col, q0, kb = parts[i]
                            done = [p[0] for p in parts]
                            n = (b * H + s) * NE + bk
                            if bk not in done[:i]:
                                at(pe, e_exped, n if s == 0 and bk == 0 and not causal else n - E_BANKS + 1)
                            kr = ks[:, s if causal else par, kb * P:(kb + 1) * P]
                            w = (S - q0) if causal else S
                            mm = pe.matmul(e_ps[:, e_bank(s, bk), col:col + w], kr, qs[:, s, q0:S], start=True, stop=True)
                            if bk not in done[i + 1:]:
                                mm.then_inc(e_scored, 1)

                        def sums():
                            bp, gp = (b, g - 1) if g else (b - 1, GROUPS - 1)
                            if not exists(bp):
                                return
                            G = bp * GROUPS + gp
                            pp = par if bp is b else 1 - par
                            if j == 0:
                                if causal:
                                    pe.wait_ge(masked, (bp * H) + gp * GH + GH)
                                else:
                                    pe.wait_ge(e_exped, (bp * H + gp * GH + GH) * NE)
                                pe.wait_ge(v_evac, (bp + 1) * NV)
                                at(pe, o_evac, G)
                            kb = j
                            q0 = kb * P if causal else 0
                            c0 = start_of[kb]
                            for hh in range(GH):
                                head = gp * GH + hh if causal else 0
                                mm = pe.matmul(o_ps[32 * hh:32 * hh + 32, 0, q0:S], vo[:, pp, kb, head, :],
                                               probs[:, gp % 2, hh, c0:c0 + S - q0], start=kb == 0, stop=kb == TB - 1)
                            if j == GH - 1:
                                mm.then_inc(pv_done, 1)

                        for step in TURNS:
                            if step == "sums":
                                sums()
                            elif step[0] == "max":
                                row_scores(step[1])
                            else:
                                exp_scores(step[1])
                        if s in V_AT[:NV] and exists(b + 1):
                            i = V_AT.index(s)
                            pe.wait_ge(xt_split, (b + 2) * KC)
                            ps = bank("x0", (v_evac, (b + 1) * NV + i + 1))
                            for t in range(TB // NV):
                                for c in range(KC):
                                    tok = slice((i * (TB // NV) + t) * P, (i * (TB // NV) + t + 1) * P)
                                    mm = product(pe, ps[:, t * VC:(t + 1) * VC], [x[:, c, tok] for x in xt],
                                                 [w[:, c, :] for w in wv], c == 0, c == KC - 1)
                            mm.then_inc(v_made, 1)
                        if s in XT_AT and exists(b + 2):
                            c = XT_AT.index(s)
                            pe.wait_ge(xn_landed, (b + 3) * DMA)
                            ps = bank("x0", (xt_split, (b + 2) * KC + c + 1))
                            for t in range(TB):
                                mm = pe.transpose(ps[:, t * P:(t + 1) * P], xn[:, t, c * P:(c + 1) * P], ident[:])
                            mm.then_inc(xt_turned, 1)
                        if QK_AT <= s < QK_AT + NQ and exists(b + 2):
                            i = s - QK_AT
                            pe.wait_ge(xt_split, (b + 3) * KC)
                            ps = bank("x0", (qk_evac, (b + 2) * NQ + i + 1))
                            n = P if causal or i < 2 else HD
                            for c in range(KC):
                                mm = product(pe, ps[0:n, :], [w[:, c, i * P:i * P + n] for w in wqk],
                                             [x[:, c, :] for x in xt], c == 0, c == KC - 1)
                            mm.then_inc(qk_made, 1)
                        if s % GH == MAX_AT:
                            bt, gt = (b, g + 1) if g + 1 < GROUPS else (b + 1, 0)
                            if exists(bt):
                                pe.wait_ge(m_reduced, (bt * H + gt * GH + GH) * NM)
                                ps = bank("x1", (mx_split, bt * GROUPS + gt + 1))
                                pe.transpose(ps[0:GH * TB, 0:P], mx[:, gt * GH * TB:(gt + 1) * GH * TB],
                                             ident[:]).then_inc(mx_turned, 1)
                        if s % GH == 2:
                            bt, gt = (b, g - 2) if g >= 2 else (b - 1, g + 2)
                            if exists(bt):
                                G = bt * GROUPS + gt
                                pe.wait_ge(o_evac, G + 1)
                                ps = bank("x1", (o_normed, G + 1))
                                for t in range(TB):
                                    mm = pe.transpose(ps[:, t * P:(t + 1) * P], osb[:, t * P:(t + 1) * P], ident[:])
                                mm.then_inc(o_turned, 1)
                        if s in OT_AT and exists(b - 1):
                            c = OT_AT.index(s)
                            pe.wait_ge(o_normed, b * GROUPS)
                            ps = bank("x1", (on_split, (b - 1) * KC + c + 1))
                            for t in range(TB):
                                mm = pe.transpose(ps[:, t * P:(t + 1) * P], on[:, t, c * P:(c + 1) * P], ident[:])
                            mm.then_inc(on_turned, 1)
                        if s in Y_AT and exists(b - 1):
                            i = Y_AT.index(s)
                            pe.wait_ge(on_split, b * KC)
                            ps = bank("x1", (y_evac, (b - 1) * 2 + i + 1))
                            for t in range(2):
                                for c in range(KC):
                                    tok = slice((2 * i + t) * P, (2 * i + t + 1) * P)
                                    mm = product(pe, ps[:, t * D:(t + 1) * D], [o[:, c, tok] for o in ot],
                                                 [w[:, c, :] for w in wo], c == 0, c == KC - 1)
                            mm.then_inc(y_made, 1)

                over_batches(pe, body, -2, (2, 14), NB)

            @block.scalar
            def _(act):
                def body(b, par=None):
                    for s in range(H):
                        g, j = divmod(s, GH)
                        if j == 0:
                            bt, gt = (b, g - 2) if g >= 2 else (b - 1, g + 2)
                            if exists(bt):
                                G = bt * GROUPS + gt
                                act.wait_ge(pv_done, G + 1)
                                at(act, o_turned, G)
                                act.activation(osb[:], o_ps[:, 0, :], ACT.Copy).then_inc(o_evac, 1)
                        if exists(b):
                            if j == 0:
                                at(act, pv_done, b * GROUPS + g - 1)
                            for c in range(NE):
                                act.wait_ge(e_scored, (b * H + s) * NE + c + 1)
                                act.activation(probs[:, g % 2, j, c * S:c * S + width[c]], e_ps[:, e_bank(s, c), 0:width[c]],
                                               ACT.Exp, scale=SCALE).then_inc(e_exped, 1)
                        if s == 0 and exists(b + 1):
                            src = rot if causal else qf
                            if causal:
                                act.wait_ge(summed, (b + 1) * 2 + 1)
                            else:
                                act.wait_ge(qk_evac, (b + 1) * NQ + 2)
                            at(act, q_written, (b + 1) * DMA)
                            act.activation(q_parts[:, 0], src[:], ACT.Copy).then_inc(q_hi, 1)
                        if s == 3 and exists(b + 1):
                            if causal:
                                act.wait_ge(summed, (b + 1) * 2 + 2)
                                at(act, k_written, (b + 1) * DMA)
                                act.activation(k_parts[:, 0], rot[:], ACT.Copy).then_inc(k_hi, 1)
                            else:
                                act.wait_ge(qk_evac, (b + 2) * NQ)
                                at(act, ks_landed, (b + 1) * 3 * DMA)
                                act.activation(k_parts[:, 0], kf[:], ACT.Copy).then_inc(k_hi, 1)
                        if s in XT_AT and exists(b + 2):
                            c = XT_AT.index(s)
                            act.wait_ge(xt_turned, (b + 2) * KC + c + 1)
                            at(act, v_made, (b + 2) * NV)
                            act.activation(xt[0][:, c, :], x0_ps[:, 0, :], ACT.Copy).then_inc(xt_hi, 1)
                        if s in OT_AT and exists(b - 1):
                            c = OT_AT.index(s)
                            act.wait_ge(on_turned, (b - 1) * KC + c + 1)
                            at(act, y_made, (b - 1) * 2)
                            act.activation(ot[0][:, c, :], x1_ps[:, 0, :], ACT.Copy).then_inc(on_hi, 1)
                        if QK_AT <= s < QK_AT + NQ and exists(b + 2):
                            i = s - QK_AT
                            act.wait_ge(qk_made, (b + 2) * NQ + i + 1)
                            if causal:
                                at(act, roped, ((b + 1) * 2 + i // 2 + 1) * 4)
                                dst, n = (qf, kf)[i // 2][:, i % 2, :], P
                            elif i < 2:
                                at(act, q_split, b + 2)
                                dst, n = qf[:, i, :], P
                            else:
                                at(act, k_split, b + 2)
                                dst, n = kf[:], HD
                            act.activation(dst, x0_ps[0:n, 0, :], ACT.Identity, bias=bqk[0:n, i:i + 1]).then_inc(qk_evac, 1)

                over_batches(act, body, -2, (2, 14), NB)

            @block.vector
            def _(dve):
                chain = Chain(dve, dve_order, 0)

                def body(b, par=None):
                    par = b % 2 if isinstance(b, int) else par

                    def normalise(i):
                        dve.wait_ge(rstd_made, (b - 1) * 2 + i + 1)
                        at(dve, stored, (b - 1) * DMA)
                        for t in range(2):
                            n = 2 * i + t
                            ins = dve.tensor_scalar(yo[:, n, :], hb[:, i, t, :], mv[:, n, 0:1], rstd[:, n:n + 1],
                                                    ALU.subtract, ALU.mult)
                        ins.then_inc(y_normed, 1)

                    def other_work(s, qb):
                        g, j = divmod(s, GH)
                        if qb == 1 and s in V_AT[:NV] and exists(b + 1):
                            i = V_AT.index(s)
                            n = TB // NV
                            dve.wait_ge(v_made, (b + 1) * NV + i + 1)
                            src = x0_ps[:, 0, 0:n * VC].rearrange("p (t h d) -> p t h d", t=n, d=HD)
                            dst = vo[:, 1 - par, i * n:(i + 1) * n, :, 0:HD]
                            bias = spread(bv[:], [[0, n], [HD, KVH], [1, HD]])
                            dve.tensor_tensor(dst, src, bias, ALU.add).then_inc(v_evac, 1)
                        if qb == (3 if causal else 2) and s in XT_AT and exists(b + 2):
                            c = XT_AT.index(s)
                            dve.wait_ge(xt_hi, (b + 2) * KC + c + 1)
                            dve.tensor_tensor(xt[1][:, c, :], x0_ps[:, 0, :], xt[0][:, c, :],
                                              ALU.subtract).then_inc(xt_split, 1)
                        if qb == 1 and s % GH == MAX_AT:
                            bt, gt = (b, g + 1) if g + 1 < GROUPS else (b + 1, 0)
                            if exists(bt):
                                G = bt * GROUPS + gt
                                dve.wait_ge(mx_turned, G + 1)
                                at(dve, max_landed, G * 2 * DMA)
                                mt = x1_ps[0:GH * TB, 0, 0:P]
                                chain.then(dve.tensor_copy(mh[:, 0, :], mt))
                                dve.tensor_tensor(mh[:, 1, :], mt, mh[:, 0, :], ALU.subtract).then_inc(mx_split, 1)
                        if qb == 2 and s % GH == 2:
                            bt, gt = (b, g - 2) if g >= 2 else (b - 1, g + 2)
                            if exists(bt):
                                dve.wait_ge(o_turned, bt * GROUPS + gt + 1)
                                o4 = x1_ps[:, 0, :].rearrange("p (t h e) -> p t h e", t=TB, h=GH)
                                sums = o4[:, :, :, HD:HD + 1].rearrange("p t h e -> p t (h e)")
                                d4 = [den[:, i, :].rearrange("p (t h) -> p t h", t=TB) for i in range(2)]
                                if causal:
                                    chain.then(dve.tensor_scalar(d4[0], sums, SUM_EPS, None, ALU.add))
                                    sums = d4[0]
                                chain.then(dve.reciprocal(d4[1], sums))
                                r = spread(den[:, 1, :], [[GH, TB], [1, GH], [0, HD]])
                                o = on[:, :, gt * GH * HD:(gt + 1) * GH * HD].rearrange("p t (h d) -> p t h d", d=HD)
                                dve.tensor_tensor(o, o4[:, :, :, 0:HD], r, ALU.mult).then_inc(o_normed, 1)
                        def lo_part(parts, whole, hi_there, split):
                            dve.wait_ge(hi_there, b + 2)
                            if len(parts.shape) == 4:
                                e = qb - 2
                                ins = dve.tensor_tensor(parts[:, 1, e], whole[:, e], parts[:, 0, e], ALU.subtract)
                            else:
                                ins = dve.tensor_tensor(parts[:, 1], whole[:], parts[:, 0], ALU.subtract)
                            if qb == 3:
                                ins.then_inc(split, 1)

                        if qb >= 2 and s == 0 and exists(b + 1):
                            lo_part(q_parts, rot if causal else qf, q_hi, q_split)
                        if qb >= (2 if causal else 3) and s == 3 and exists(b + 1):
                            lo_part(k_parts, rot if causal else kf, k_hi, k_split)
                        if qb == 1 and s in OT_AT and exists(b - 1):
                            c = OT_AT.index(s)
                            dve.wait_ge(on_hi, (b - 1) * KC + c + 1)
                            dve.tensor_tensor(ot[1][:, c, :], x1_ps[:, 0, :], ot[0][:, c, :],
                                              ALU.subtract).then_inc(on_split, 1)
                        if qb in (2, 3) and s in Y_AT and exists(b - 1):
                            i = Y_AT.index(s)
                            if qb == 2:
                                dve.wait_ge(y_made, (b - 1) * 2 + i + 1)
                                at(dve, y_normed, (b - 2) * 2 + i + 1)
                                dve.wait_ge(xr_biased, b)
                                src = x1_ps[:, 0, :].rearrange("p (t d) -> p t d", t=2)
                                dve.tensor_tensor(hb[:, i], src, xr[:, 2 * i:2 * i + 2, :], ALU.add).then_inc(y_evac, 1)
                            else:
                                dve.wait_ge(y_evac, (b - 1) * 2 + i + 1)
                                dve.bn_stats(stats[:, 2 * i, :], hb[:, i, 0, :])
                                chain.then(dve.bn_stats(stats[:, 2 * i + 1, :], hb[:, i, 1, :]), dve_passed)
                                dve.bn_aggr(mv[:, 2 * i, :], stats[:, 2 * i, :])
                                chain.then(dve.bn_aggr(mv[:, 2 * i + 1, :], stats[:, 2 * i + 1, :]))
                                dve.tensor_scalar(veps[:, 2 * i:2 * i + 2],
                                                  mv[:, 2 * i:2 * i + 2, 1:2].rearrange("p t e -> p (t e)"),
                                                  LN_EPS, None, ALU.add).then_inc(var_made, 1)

                        if causal and qb == 3 and s in (13, 14) and exists(b - 1):
                            normalise(s - 13)

                    if isinstance(b, int) and b == -2:
                        dve.memset(ks[:].bitcast(F32), -1.0).then_inc(ks_filled, 1)
                    if isinstance(b, int) and b == -1:
                        dve.wait_ge(const_made, CONSTS)

                    for s in range(H):
                        bm, hm = (b, s + LEAD) if s + LEAD < H else (b + 1, s + LEAD - H)
                        for qb in range(TB):
                            if s:
                                other_work(s - 1, qb)
                            if exists(bm):
                                part, first = row_parts[qb]
                                n = (bm * H + hm) * NM + part
                                if causal:
                                    if first == 0:
                                        at(dve, m_reduced, n - NM + 1)
                                        at_alone(dve, m_scored, n + 1, dve_passed)
                                else:
                                    dve.wait_ge(m_scored, n + 1)
                                w = (qb + 1) * P if causal else S
                                col = mx[:, hm * TB + qb:hm * TB + qb + 1]
                                scores = m_ps[:, m_bank(part), first:first + w]
                                if causal:
                                    ins = dve.tensor_tensor_reduce(junk[:, S * part + first:S * part + first + w], scores,
                                                                   mask[:, S - w:S], 1.0, MASKED, ALU.add, ALU.max, col)
                                else:
                                    ins = dve.tensor_reduce(col, scores, AX.X, ALU.max)
                                if last_of_part[qb]:
                                    ins.then_inc(m_reduced, 1)

                chain.per_two = 2 * (GROUPS * (3 if causal else 2) + 2 * 2)
                over_batches(dve, body, -2, (2, 14), NB, chain)

            @block.gpsimd
            def _(pool):
                pool.memset(mhalf[:], -0.5)
                pool.memset(vo[:], 0.0).then_inc(const_made, 1)
                pool.wait_ge(const_made, 1)
                pool.memset(vo[:, :, :, :, HD:HD + 1], 1.0)
                if causal:
                    pool.memset(mask[:], 0.0).then_inc(const_made, 1)
                    pool.wait_ge(const_made, 2)
                    pool.affine_select(out=mask[:], in_=mask[:], pattern=[[-1, S]], compare_op=ALU.is_ge,
                                       fill=MASKED, base=384, channel_multiplier=1)
                pool.memset(qs[:].bitcast(F32), 0.0).then_inc(const_made, 1)

                def body(b, par=None):
                    for s in range(H):
                        g, j = divmod(s, GH)
                        if causal and exists(b):
                            at_alone(pool, e_exped, (b * H + s + 1) * NE, pool_passed)
                            for kbs, step in (((0, 1, 2), 512), ((3,), 0)):
                                starts = sorted(start_of[kb] for kb in range(TB))
                                first = 896 if len(kbs) == 1 else 0
                                dims = [[512, 3], [1, P]] if first == 0 else [[1, P]]
                                blk = spread(probs[:, g % 2, j, first:first + 1], dims)
                                pattern = [[0, 3], [1, P]] if first == 0 else [[1, P]]
                                ins = pool.affine_select(out=blk, in_=blk, pattern=pattern, compare_op=ALU.is_ge,
                                                         fill=0.0, base=0, channel_multiplier=-1)
                            ins.then_inc(masked, 1)
                        if causal:
                            for slot, which, ahead, part in ((12, 0, 2, 0), (13, 0, 2, 1), (15, 1, 2, 0), (0, 1, 1, 1)):
                                bt = b + ahead
                                if s == slot and exists(bt):
                                    src = (qf, kf)[which]
                                    if part == 0:
                                        pool.wait_ge(qk_evac, bt * NQ + 2 * which + 2)
                                        at(pool, summed, bt * 2 + which)
                                    for e in range(2):
                                        pool.tensor_tensor(prods[:, 2 * part + e, :], src[:, e, :],
                                                           cs[:, (e + part) % 2, :], ALU.mult).then_inc(roped, 1)
                            for slot, which, ahead in ((14, 0, 2), (1, 1, 1)):
                                bt = b + ahead
                                if s == slot and exists(bt):
                                    pool.wait_ge(roped, (bt * 2 + which + 1) * 4)
                                    at(pool, *((q_split, bt + 1) if which else (k_split, bt)))
                                    pool.tensor_tensor(rot[:, 0, :], prods[:, 0, :], prods[:, 1, :], ALU.subtract)
                                    pool.tensor_tensor(rot[:, 1, :], prods[:, 2, :], prods[:, 3, :],
                                                       ALU.add).then_inc(summed, 1)
                        if s == 8 and exists(b - 1):
                            pool.wait_ge(xr_landed, b * DMA)
                            pool.tensor_tensor(xr[:], xr[:], spread(bo[:], [[0, TB], [1, D]]), ALU.add).then_inc(xr_biased, 1)
                        if s in Y_AT and exists(b - 1):
                            i = Y_AT.index(s)
                            n = (b - 1) * 2 + i
                            pool.wait_ge(var_made, n + 1)
                            at(pool, y_normed, n - 1)
                            half = slice(2 * i, 2 * i + 2)
                            pool.tensor_tensor(rstd[:, half], veps[:, half], mhalf[:], ALU.pow).then_inc(rstd_made, 1)
                            if not causal:
                                at(pool, stored, (b - 1) * DMA)
                                pool.tensor_tensor(yo[:, half], hb[:, i], spread(mv[:, 2 * i:2 * i + 1, :], [[2, 2], [0, D]]),
                                                   ALU.subtract).then_inc(rstd_made, 1)
                                pool.wait_ge(rstd_made, 2 * (n + 1))
                                pool.tensor_tensor(yo[:, half], yo[:, half], spread(rstd[:, half], [[1, 2], [0, D]]),
                                                   ALU.mult).then_inc(y_normed, 1)

                over_batches(pool, body, -2, (2, 14), NB)

            @block.sync
            def _(sp):
                def rows(x, b):
                    return x[bass.ds(b, 1)].rearrange("o (t p) d -> p (o t) d", p=P)

                def body(b, par=None):
                    par = b % 2 if isinstance(b, int) else par
                    if isinstance(b, int) and b == -1:
                        sp.wait_ge(const_made, CONSTS)
                        sp.wait_ge(ks_filled, 1)

                    for s in range(H):
                        g = s // GH
                        if s % GH == MAX_AT:
                            bt, gt = (b, g + 1) if g + 1 < GROUPS else (b + 1, 0)
                            if exists(bt):
                                sp.wait_ge(mx_split, bt * GROUPS + gt + 1)
                                for r in range(2):
                                    sp.dma_start(qs[MAX_ROW + r:MAX_ROW + r + 1, gt * GH:(gt + 1) * GH, :].bitcast(F32),
                                                 mh[:, r, :].bitcast(F32)).then_inc(max_landed, DMA)
                        if s == (1 if causal else 4) and exists(b + 2):
                            at(sp, xt_turned, (b + 2) * KC)
                            sp.dma_start(xn[:], rows(x_in, b + 2)).then_inc(xn_landed, DMA)
                        if s == 1 and exists(b + 1):
                            sp.wait_ge(q_split, b + 2)
                            sp.dma_start(q_dram[bass.ds(b + 1, 1)].rearrange("o r (e i) h t -> (o i h) (r e) t", e=2),
                                         q_parts.rearrange("p r e t -> p (r e) t").bitcast(F32)).then_inc(q_written, DMA)
                        if s == 4 and exists(b + 1):
                            sp.wait_ge(k_split, b + 2)
                            if causal:
                                sp.dma_start(k_dram[bass.ds(b + 1, 1)].rearrange("o r (e i) h t -> (o i h) (r e) t", e=2),
                                             k_parts.rearrange("p r e t -> p (r e) t").bitcast(F32)).then_inc(k_written, DMA)
                                sp.wait_ge(k_written, (b + 2) * DMA)
                            else:
                                at(sp, e_scored, b * H * NE)
                                for n, r in enumerate((0, 1, 0)):
                                    sp.dma_start(ks[n * HD:(n + 1) * HD, 1 - par, :].bitcast(F32),
                                                 k_parts[:, r, :].bitcast(F32)).then_inc(ks_landed, DMA)
                            sp.wait_ge(q_written, (b + 2) * DMA)
                        if s in (4, 7, 11, 15) and exists(b + 1):
                            gt = (4, 7, 11, 15).index(s)
                            at(sp, e_scored, (b * H + gt * GH + GH) * NE)
                            hs = slice(gt * GH, (gt + 1) * GH)
                            for n, (rq, rk) in enumerate(((0, 0), (0, 1), (1, 0))):
                                for dram, stack, r in ((q_dram, qs, rq), (k_dram, ks, rk))[:2 if causal else 1]:
                                    sp.dma_start(stack[n * HD:(n + 1) * HD, hs, :].bitcast(F32),
                                                 dram[bass.ds(b + 1, 1), r, :, hs, :].rearrange("o d h t -> (o d) h t")
                                                 ).then_inc(stack_landed[gt], DMA)
                        if s == 5 and exists(b - 1):
                            at(sp, y_evac, (b - 1) * 2)
                            sp.dma_start(xr[:], rows(x_in, b - 1)).then_inc(xr_landed, DMA)
                        if s == 15 and exists(b - 1):
                            sp.wait_ge(y_normed, b * 2)
                            sp.dma_start(rows(x_out, b - 1), yo[:]).then_inc(stored, DMA)

                over_batches(sp, body, -2, (2, 14), NB)
                sp.wait_ge(stored, NB * DMA)


def expert_layer(nc, sems, weights, passed, name, x_in, x_out, gate, up_w, down_w, E, TOP, plain, glu, ident_in):
    U = plain + glu
    scaled = TOP == 1
    kinds = ["plain"] * plain + ["glu"] * glu
    DC = [2] * plain + [1] * glu
    d_first = [sum(DC[:u]) for u in range(U)]
    PAD = 8
    with ExitStack() as ctx:
        def sb(n, shape, dt=F32):
            return ctx.enter_context(nc.sbuf_tensor(f"{name}_{n}", shape, dt))

        def sem(n):
            return sems.enter_context(nc.semaphore(f"{name}_{n}"))

        w1 = [sb(f"w_up_{p}", [P, U, KC, 2 * P], F32R) for p in ("hi", "lo")]
        w2 = [sb(f"w_down_{p}", [P, sum(DC), D], F32R) for p in ("hi", "lo")]
        wg = [sb(f"w_gate_{p}", [P, KC, E], F32R) for p in ("hi", "lo")]
        xn2 = sb("x", [P, 2, TB, D])
        xt2 = [sb(f"xT_{p}", [P, 2, KC, S], F32R) for p in ("hi", "lo")]
        hf = sb("h", [P, 2 * S])
        ht = [sb(f"hT_{p}", [P, 2, 2 * S], F32R) for p in ("hi", "lo")]
        acc2 = sb("acc", [P, 2, TB, D])
        yo = sb("y_out", [P, TB, D])
        ident = sb("identity", [P, P])
        lg = sb("logits", [P, TB, E + PAD])
        left = sb("logits_left", [P, TB, E + PAD])
        top8 = sb("top8", [P, TB, 8])
        top = sb("to_replace", [P, TB, 8])
        low = sb("shifted", [P, TB, E])
        ex = sb("exps", [P, TB, E])
        wt2 = sb("weights", [P, 2, TB, E])
        tot = sb("totals", [P, 2, TB])
        stats = sb("stats", [P, TB, 6])
        mv = sb("mean_var", [P, TB, 2])
        veps = sb("var_eps", [P, TB])
        rstd = sb("rstd", [P, TB])
        mhalf = sb("minus_half", [P, TB])
        xs = sb("x_scaled", [P, TB, D]) if scaled else None

        def psum(n, banks):
            return ctx.enter_context(nc.psum_tensor(f"{name}_{n}", [P, banks, S], F32))

        h_ps = [psum("ps_h0", 2), psum("ps_h1", 2)]
        y_ps = psum("ps_y", 2)
        t_ps = psum("ps_turn", 2)

        const_landed, const_made = sem("const_landed"), sem("const_made")
        x_landed, stored = sem("x_landed"), sem("stored")
        x_turned, xt_hi, xt_split = sem("x_turned"), sem("xt_hi"), sem("xt_split")
        routed, logits_read, shifted, exped, weighed, x_scaled = (
            sem("routed"), sem("logits_read"), sem("shifted"), sem("exped"), sem("weighed"), sem("x_scaled"))
        h_made, h_silu, h_whole, h_hi, h_split = (
            sem("h_made"), sem("h_silu"), sem("h_whole"), sem("h_hi"), sem("h_split"))
        y_made, y_added, var_made, rstd_made, y_normed = (
            sem("y_made"), sem("y_added"), sem("var_made"), sem("rstd_made"), sem("y_normed"))
        dve_order, scale_made = sem("dve_order"), sem("scale_made") if scaled else None
        dve_passed, pool_passed = passed

        turns = 2 * KC if scaled else KC
        TURN_AT, ROUTE_AT, WEIGH_AT, SCALED_AT = 1, 3, 4, 6

        stage = [t[:, i].rearrange("p t d -> p (t d)") for t in (xn2, acc2) for i in range(2)]
        specs = [(gate, *[w.rearrange("p c n -> p (c n)") for w in wg])]
        for u in range(0, U, 2):
            specs.append((up_w[u:u + 2].rearrange("u p n -> p u n"),
                          *[w[:, u:u + 2].rearrange("p u c n -> p u (c n)") for w in w1]))
            d0, d1 = d_first[u], d_first[u + 1] + DC[u + 1]
            specs.append((down_w[:, d0:d1, :], *[w[:, d0:d1, :] for w in w2]))
        weights.load(specs, stage, [(ident[:], ident_in)], const_landed)

        with nc.Block() as block:
            @block.gpsimd
            def _(pool):
                pool.memset(mhalf[:], -0.5)
                pool.memset(lg[:], MASKED)

            @block.vector
            def _(dve):
                dve.memset(top[:], MASKED)

        def unit(b, u):
            return b * U + u

        with nc.Block() as block:
            @block.tensor
            def _(pe):
                def turn(b, n, src):
                    at(pe, xt_split, b * turns + n - 1)
                    for t in range(TB):
                        mm = pe.transpose(t_ps[:, n % 2, t * P:(t + 1) * P], src[:, t, (n % KC) * P:(n % KC + 1) * P],
                                          ident[:])
                    mm.then_inc(x_turned, 1)

                def turn_x(b, par):
                    pe.wait_ge(x_landed, (b + 1) * DMA)
                    at(pe, logits_read, b)
                    for c in range(KC):
                        turn(b, c, xn2[:, par])

                def route(b, par):
                    pe.wait_ge(xt_split, b * turns + KC)
                    for t in range(TB):
                        for c in range(KC):
                            mm = product(pe, t_ps[:, 0, t * E:(t + 1) * E],
                                         [x[:, par, c, t * P:(t + 1) * P] for x in xt2],
                                         [w[:, c, :] for w in wg], c == 0, c == KC - 1)
                    mm.then_inc(routed, 1)

                def turn_scaled(b):
                    pe.wait_ge(x_scaled, b + 1)
                    pe.wait_ge(logits_read, b + 1)
                    for c in range(KC):
                        turn(b, KC + c, xs)

                def up(b, u, par):
                    n = unit(b, u)
                    if u == 0:
                        pe.wait_ge(xt_split, (b + 1) * turns)
                    at(pe, h_split, n - 1)
                    for m in range(2):
                        for c in range(KC):
                            mm = product(pe, h_ps[u % 2][:, m, :], [w[:, u, c, m * P:(m + 1) * P] for w in w1],
                                         [x[:, par, c, :] for x in xt2], c == 0, c == KC - 1)
                    mm.then_inc(h_made, 1)

                def down(b, u):
                    n = unit(b, u)
                    pe.wait_ge(h_split, n + 1)
                    for i in range(2):
                        at(pe, y_added, 2 * n + i - 1)
                        for t in range(2):
                            tok = (2 * i + t) * P
                            for c in range(DC[u]):
                                mm = product(pe, y_ps[:, i, t * D:(t + 1) * D],
                                             [h[:, u % 2, c * S + tok:c * S + tok + P] for h in ht],
                                             [w[:, d_first[u] + c, :] for w in w2], c == 0, c == DC[u] - 1)
                        mm.then_inc(y_made, 1)

                def body(b, par=None):
                    par = b % 2 if isinstance(b, int) else par
                    if exists(b):
                        for u in range(U):
                            up(b, u, par)
                            if u == TURN_AT and exists(b + 1):
                                turn_x(b + 1, 1 - par)
                            if u == ROUTE_AT and exists(b + 1):
                                route(b + 1, 1 - par)
                            if u == SCALED_AT and scaled and exists(b + 1):
                                turn_scaled(b + 1)
                            if u or exists(b - 1):
                                down(*((b, u - 1) if u else (b - 1, U - 1)))
                    elif b < 0:
                        turn_x(0, 0)
                        route(0, 0)
                        if scaled:
                            turn_scaled(0)
                    else:
                        down(b - 1, U - 1)

                over_batches(pe, body, -1, (2, 14), NB)

            @block.scalar
            def _(act):
                def hi_parts(b, par, chunks):
                    for n in chunks:
                        act.wait_ge(x_turned, b * turns + n + 1)
                        if n == 0:
                            at(act, h_made, unit(b - 1, 0))
                        if n == KC:
                            act.wait_ge(routed, b + 1)
                        act.activation(xt2[0][:, par, n % KC, :], t_ps[:, n % 2, :], ACT.Copy).then_inc(xt_hi, 1)

                def exponentials(b):
                    act.wait_ge(shifted, b + 1)
                    n = E if TOP > 1 else 1
                    act.activation(ex[:, :, 0:n], low[:, :, 0:n], ACT.Exp).then_inc(exped, 1)

                def hidden(b, u):
                    n = unit(b, u)
                    act.wait_ge(h_made, n + 1)
                    w = 2 * S if kinds[u] == "plain" else S
                    at(act, h_split, n)
                    act.activation(hf[:, 0:w], h_ps[u % 2].rearrange("p m s -> p (m s)")[:, 0:w],
                                   ACT.Silu).then_inc(h_silu, 1)
                    if kinds[u] == "glu":
                        act.wait_ge(h_whole, b * glu + (u - plain) + 1)
                    else:
                        act.wait_ge(h_silu, n + 1)
                    at(act, y_made, 2 * (n - 1))
                    act.activation(ht[0][:, u % 2, 0:w], hf[:, 0:w], ACT.Copy).then_inc(h_hi, 1)

                def body(b, par=None):
                    par = b % 2 if isinstance(b, int) else par
                    if exists(b):
                        for u in range(U):
                            hidden(b, u)
                            if u == TURN_AT and exists(b + 1):
                                hi_parts(b + 1, 1 - par, range(KC))
                            if u == WEIGH_AT and exists(b + 1):
                                exponentials(b + 1)
                            if u == SCALED_AT and scaled and exists(b + 1):
                                hi_parts(b + 1, 1 - par, range(KC, turns))
                    elif b < 0:
                        hi_parts(0, 0, range(KC))
                        exponentials(0)
                        hi_parts(0, 0, range(KC, turns))

                over_batches(act, body, -1, (2, 14), NB)

            @block.vector
            def _(dve):
                chain = Chain(dve, dve_order, 0)

                def lo_parts(b, par, chunks):
                    for n in chunks:
                        dve.wait_ge(xt_hi, b * turns + n + 1)
                        dve.tensor_tensor(xt2[1][:, par, n % KC, :], t_ps[:, n % 2, :], xt2[0][:, par, n % KC, :],
                                          ALU.subtract).then_inc(xt_split, 1)

                def choose(b):
                    dve.wait_ge(routed, b + 1)
                    dve.tensor_copy(lg[:, :, 0:E], t_ps[:, 0, 0:TB * E].rearrange("p (t e) -> p t e", t=TB)
                                    ).then_inc(logits_read, 1)
                    at_alone(dve, logits_read, b + 1, dve_passed)
                    for t in range(TB):
                        ins = dve.max(top8[:, t, :], lg[:, t, 0:E])
                    chain.then(ins)
                    chain.then(dve.tensor_copy(top[:, :, 0:TOP], top8[:, :, 0:TOP]), dve_passed)
                    for t in range(TB):
                        ins = dve.match_replace(left[:, t, :], top[:, t, :], lg[:, t, :], -3.3e38)
                    chain.then(ins)
                    if TOP > 1:
                        biggest = spread(top8[:], [[8, TB], [0, E]])
                        dve.tensor_tensor(low[:], lg[:, :, 0:E], biggest, ALU.subtract).then_inc(shifted, 1)
                    else:
                        dve.tensor_scalar(low[:, :, 0:1], top8[:, :, 0:1], -1.0, None, ALU.mult).then_inc(shifted, 1)

                def weigh(b, par):
                    wt = wt2[:, par]
                    chosen = dve.tensor_tensor(wt, left[:, :, 0:E], lg[:, :, 0:E], ALU.not_equal)
                    if TOP > 1:
                        chain.then(chosen)
                        dve.wait_ge(exped, b + 1)
                        chain.then(dve.tensor_tensor(wt, wt, ex[:], ALU.mult))
                        chain.then(dve.tensor_reduce(tot[:, 0, :], wt, AX.X, ALU.add))
                        chain.then(dve.reciprocal(tot[:, 1, :], tot[:, 0, :]))
                        dve.tensor_tensor(wt, wt, spread(tot[:, 1, :], [[1, TB], [0, E]]),
                                          ALU.mult).then_inc(weighed, 1)
                    else:
                        chosen.then_inc(weighed, 1)
                        dve.wait_ge(exped, b + 1)
                        chain.then(dve.tensor_scalar(tot[:, 0, :], ex[:, :, 0:1].rearrange("p t e -> p (t e)"),
                                                     1.0, None, ALU.add))
                        at(dve, x_scaled, b)
                        dve.reciprocal(tot[:, 1, :], tot[:, 0, :]).then_inc(scale_made, 1)

                def gated(b, u):
                    if kinds[u] == "glu":
                        dve.wait_ge(h_silu, unit(b, u) + 1)
                        dve.tensor_tensor(hf[:, 0:S], hf[:, 0:S], h_ps[u % 2][:, 1, :], ALU.mult).then_inc(h_whole, 1)

                def hidden_lo(b, u):
                    n = unit(b, u)
                    w = 2 * S if kinds[u] == "plain" else S
                    dve.wait_ge(h_hi, n + 1)
                    dve.tensor_tensor(ht[1][:, u % 2, 0:w], hf[:, 0:w], ht[0][:, u % 2, 0:w],
                                      ALU.subtract).then_inc(h_split, 1)

                def add_up(b, u, par, i):
                    n = unit(b, u)
                    if i == 0 and u == 0:
                        dve.wait_ge(weighed, b + 1)
                    elif i == 0:
                        dve.wait_ge(y_added, 2 * n)
                    dve.wait_ge(y_made, 2 * n + i + 1)
                    for t in range(2):
                        k = 2 * i + t
                        weight = wt2[:, par, k, u:u + 1] if u < E else 1.0
                        ins = dve.scalar_tensor_tensor(out=acc2[:, par, k, :], in0=y_ps[:, i, t * D:(t + 1) * D],
                                                       scalar=weight, in1=(acc2 if u else xn2)[:, par, k, :],
                                                       op0=ALU.mult, op1=ALU.add)
                    ins.then_inc(y_added, 1)

                def moments(b, par):
                    dve.wait_ge(y_added, (b + 1) * U * 2)
                    at(dve, y_normed, b)
                    for t in range(TB):
                        ins = dve.bn_stats(stats[:, t, :], acc2[:, par, t, :])
                    chain.then(ins, dve_passed)
                    for t in range(TB):
                        ins = dve.bn_aggr(mv[:, t, :], stats[:, t, :])
                    chain.then(ins)
                    dve.tensor_scalar(veps[:], mv[:, :, 1:2].rearrange("p t e -> p (t e)"), LN_EPS, None,
                                      ALU.add).then_inc(var_made, 1)

                def body(b, par=None):
                    par = b % 2 if isinstance(b, int) else par
                    if exists(b):
                        for u in range(U):
                            gated(b, u)
                            before = (b, u - 1, par) if u else (b - 1, U - 1, 1 - par)
                            if exists(before[0]):
                                add_up(*before, 0)
                            hidden_lo(b, u)
                            if u == TURN_AT and exists(b + 1):
                                lo_parts(b + 1, 1 - par, range(KC))
                            if u == ROUTE_AT and exists(b + 1):
                                choose(b + 1)
                            if u == WEIGH_AT and exists(b + 1):
                                weigh(b + 1, 1 - par)
                            if u == SCALED_AT and scaled and exists(b + 1):
                                lo_parts(b + 1, 1 - par, range(KC, turns))
                            if exists(before[0]):
                                add_up(*before, 1)
                            if u == 0 and exists(b - 1):
                                moments(b - 1, 1 - par)
                    elif b < 0:
                        lo_parts(0, 0, range(KC))
                        choose(0)
                        weigh(0, 0)
                        lo_parts(0, 0, range(KC, turns))
                    else:
                        for i in range(2):
                            add_up(b - 1, U - 1, 1 - par, i)
                        moments(b - 1, 1 - par)

                chain.per_two = 2 * ((7 if TOP > 1 else 4) + 2)
                over_batches(dve, body, -1, (2, 14), NB, chain)

            @block.gpsimd
            def _(pool):
                def body(b, par=None):
                    par = b % 2 if isinstance(b, int) else par
                    if exists(b - 1):
                        pool.wait_ge(var_made, b)
                        at(pool, y_normed, b - 1)
                        pool.tensor_tensor(rstd[:], veps[:], mhalf[:], ALU.pow).then_inc(rstd_made, 1)
                        at(pool, stored, (b - 1) * DMA)
                        pool.tensor_tensor(yo[:], acc2[:, 1 - par], spread(mv[:], [[2, TB], [0, D]]),
                                           ALU.subtract).then_inc(rstd_made, 1)
                        pool.wait_ge(rstd_made, 2 * b)
                        pool.tensor_tensor(yo[:], yo[:], spread(rstd[:], [[1, TB], [0, D]]),
                                           ALU.mult).then_inc(y_normed, 1)
                    if scaled and exists(b + 1):
                        pool.wait_ge(scale_made, b + 2)
                        at(pool, x_turned, (b + 1) * turns)
                        pool.tensor_tensor(xs[:], xn2[:, 1 - par], spread(tot[:, 1, :], [[1, TB], [0, D]]),
                                           ALU.mult).then_inc(x_scaled, 1)

                over_batches(pool, body, -1, (2, 14), NB)

            @block.sync
            def _(sp):
                def rows(x, b):
                    return x[bass.ds(b, 1)].rearrange("o (t p) d -> p (o t) d", p=P)

                def body(b, par=None):
                    par = b % 2 if isinstance(b, int) else par
                    if exists(b + 1):
                        at(sp, y_added, unit(b - 1, 0) * 2 + 2)
                        at(sp, x_landed, (b + 1) * DMA)
                        sp.dma_start(xn2[:, 1 - par], rows(x_in, b + 1)).then_inc(x_landed, DMA)
                    if exists(b - 1):
                        sp.wait_ge(y_normed, b)
                        sp.dma_start(rows(x_out, b - 1), yo[:]).then_inc(stored, DMA)

                over_batches(sp, body, -1, (2, 14), NB)
                sp.wait_ge(stored, NB * DMA)


def phase(nc, sems, weights, passed, which, x, out, a):
    if which == "a0":
        attention_layer(nc, sems, weights, passed, "l0", True, x, out, (a["l0_wqk"], a["l0_wv"]), (a["l0_bqk"], a["l0_bv"]),
                        a["l0_wo"], a["l0_bo"], (a["cos_sin"],), a["ident"])
    if which == "e0":
        expert_layer(nc, sems, weights, passed, "e0", x, out, a["e0_gate"], a["e0_up"], a["e0_down"], 16, 4, 16, 2, a["ident"])
    if which == "a1":
        attention_layer(nc, sems, weights, passed, "l1", False, x, out, (a["l1_wqk"], a["l1_wv"]), (a["l1_bqk"], a["l1_bv"]),
                        a["l1_wo"], a["l1_bo"], (), a["ident"])
    if which == "e1":
        expert_layer(nc, sems, weights, passed, "e1", x, out, a["e1_gate"], a["e1_up"], a["e1_down"], 8, 1, 0, 8, a["ident"])


def program(nc, x, out, a):
    between = [nc.dram_tensor(n, [NB, S, D], F32, kind="Internal").ap() for n in ("x1", "x2", "x3")]
    stops = [x, *between, out]
    with ExitStack() as sems:
        weights = WeightLoads(nc, sems)
        passed = [sems.enter_context(nc.semaphore(n)) for n in ("dve_passed", "pool_passed")]
        for n, which in enumerate(("a0", "e0", "a1", "e1")):
            phase(nc, sems, weights, passed, which, stops[n], stops[n + 1], a)


def layouts(i):
    f = {k: np.asarray(v) for k, v in i.items()}

    def chunks(w):
        return np.ascontiguousarray(w.reshape(KC, P, -1).transpose(1, 0, 2).reshape(P, -1))

    def rowwise(v, n=P):
        return np.ascontiguousarray(np.broadcast_to(v.reshape(1, -1), (n, v.size)))

    order = np.arange(D).reshape(H, HALF, 2).transpose(2, 1, 0).reshape(-1)
    one_head = np.arange(HD).reshape(HALF, 2).T.reshape(-1)
    wt = f["L0_attn_w_qkv"].T
    bq = f["L0_attn_b_qkv"]
    a = {
        "l0_wqk": chunks(np.concatenate([wt[:, :D][:, order], wt[:, D:2 * D][:, order]], 1)),
        "l0_wv": chunks(wt[:, 2 * D:]),
        "l0_bqk": np.ascontiguousarray(np.concatenate([bq[:D][order], bq[D:2 * D][order]]).reshape(4, P).T),
        "l0_bv": rowwise(bq[2 * D:]),
        "l0_wo": chunks(f["L0_attn_w_out"].T),
        "l0_bo": rowwise(f["L0_attn_b_out"]),
    }
    a["l1_wqk"] = chunks(np.concatenate([f["L1_attn_Wq"][:, order], f["L1_attn_Wk"][:, one_head]], 1))
    a["l1_wv"] = chunks(f["L1_attn_Wv"])
    pad = np.zeros(P - HD, np.float32)
    a["l1_bqk"] = np.ascontiguousarray(np.concatenate([f["L1_attn_bq"][order], f["L1_attn_bk"][one_head], pad]).reshape(3, P).T)
    a["l1_bv"] = rowwise(f["L1_attn_bv"])
    a["l1_wo"] = chunks(f["L1_attn_Wo"])
    a["l1_bo"] = rowwise(f["L1_attn_bo"])
    gu = f["L0_ffn_shared_gu"].T
    shared = [np.concatenate([gu[:, u * P:(u + 1) * P], gu[:, D + u * P:D + (u + 1) * P]], 1) for u in range(2)]
    a["e0_gate"] = chunks(f["L0_ffn_gate_w"].T)
    a["e0_up"] = np.stack([chunks(w.T) for w in f["L0_ffn_w1"]] + [chunks(w) for w in shared])
    down = np.concatenate([w.T for w in f["L0_ffn_w2"]] + [f["L0_ffn_shared_down"].T], 0)
    a["e0_down"] = np.ascontiguousarray(down.reshape(-1, P, D).transpose(1, 0, 2))
    a["e1_gate"] = chunks(f["L1_ffn_gate_w"].T)
    a["e1_up"] = np.stack([chunks(np.concatenate([g.T, u.T], 1)) for g, u in zip(f["L1_ffn_w_gate"], f["L1_ffn_w_up"])])
    a["e1_down"] = np.ascontiguousarray(f["L1_ffn_w_down"].transpose(2, 0, 1))
    inv = (10000.0 ** (-np.arange(0, HD, 2, dtype=np.float32) / HD)).astype(np.float32)
    ang = np.arange(S, dtype=np.float32)[None, :] * inv[:, None]
    a["cos_sin"] = np.repeat(np.stack([np.cos(ang), np.sin(ang)], 1), H, 0).astype(np.float32)
    a["ident"] = np.eye(P, dtype=np.float32)
    return a


def kernel(**inputs):
    import concourse.bacc as bacc
    from concourse.bass_utils import run_bass_kernel_spmd

    nc = bacc.Bacc("TRN2", target_bir_lowering=False, num_devices=1, dynamic_dma_scratch_size=64)
    arrays = {"x": np.ascontiguousarray(inputs["L0_attn_x"]), **layouts(inputs)}
    aps = {n: nc.dram_tensor(n, list(v.shape), F32, kind="ExternalInput").ap() for n, v in arrays.items()}
    out = nc.dram_tensor("out", [NB, S, D], F32, kind="ExternalOutput").ap()
    program(nc, aps.pop("x"), out, aps)
    r = run_bass_kernel_spmd(nc, [arrays], core_ids=[0])
    return r.results[0]["out"]
```
